# Optimizing a Trainium2 kernel written in Bass

```python
import numpy as np
import jax
import jax.numpy as jnp

def _softmax(x, axis=-1):
    return jax.nn.softmax(x, axis=axis)

def _gelu(x):
    return jax.nn.gelu(x, approximate=True)

def _silu(x):
    return jax.nn.silu(x)

def _sigmoid(x):
    return jax.nn.sigmoid(x)

def _layernorm(x, axis=-1, eps=1e-05):
    m = jnp.mean(x, axis=axis, keepdims=True)
    v = jnp.var(x, axis=axis, keepdims=True)
    return (x - m) / jnp.sqrt(v + eps)

def _scatter_add(tgt, idx, src, axis=0):
    return tgt.at[idx].add(src)

def _segment_sum(src, seg, n):
    return jax.ops.segment_sum(src, seg, n)
kernel_name = 'mk_sandwich_d2_jaxref_r8_413630'

def setup_inputs(seed: int=0):
    np.random.seed(seed)
    _w = jnp.asarray

    def _L0_attn_setup():
        import jax, jax.numpy as jnp
        import numpy as np
        BLOCK_H = 32
        BLOCK_W = 32
        N_FEAT = 512
        K_FEAT = 512
        key = jax.random.key(seed)
        k1, k2, k3 = jax.random.split(key, 3)
        data = jax.random.normal(k1, (4, 128, K_FEAT), dtype=jnp.float32)
        weight = jax.random.normal(k2, (N_FEAT, K_FEAT), dtype=jnp.float32) * 0.02
        nb, kb = (N_FEAT // BLOCK_H, K_FEAT // BLOCK_W)
        block_pattern = jax.random.randint(k3, (nb, kb), 0, 2, dtype=jnp.int32)
        mask = jnp.repeat(jnp.repeat(block_pattern, BLOCK_H, axis=0), BLOCK_W, axis=1)
        return {'data': data, 'weight': weight, 'mask': mask}
    _L0_attn_in = _L0_attn_setup()

    def _L0_ffn_setup():
        import jax, jax.numpy as jnp
        import numpy as np
        HIDDEN = 512
        INTER = 1376
        BATCH, SEQ = (2, 256)
        key = jax.random.key(seed)
        ks = jax.random.split(key, 7)
        s_h = 1.0 / np.sqrt(HIDDEN)
        s_i = 1.0 / np.sqrt(INTER)
        return {'hidden_states': jax.random.normal(ks[0], (BATCH, SEQ, HIDDEN), dtype=jnp.float32), 'w_gate': jax.random.uniform(ks[1], (INTER, HIDDEN), jnp.float32, -s_h, s_h), 'b_gate': jax.random.uniform(ks[2], (INTER,), jnp.float32, -s_h, s_h), 'w_up': jax.random.uniform(ks[3], (INTER, HIDDEN), jnp.float32, -s_h, s_h), 'b_up': jax.random.uniform(ks[4], (INTER,), jnp.float32, -s_h, s_h), 'w_down': jax.random.uniform(ks[5], (HIDDEN, INTER), jnp.float32, -s_i, s_i), 'b_down': jax.random.uniform(ks[6], (HIDDEN,), jnp.float32, -s_i, s_i)}
    _L0_ffn_in = _L0_ffn_setup()

    def _L1_attn_setup():
        import jax, jax.numpy as jnp
        import numpy as np
        H = 512
        D = H // 4
        key = jax.random.key(seed)
        k1, k2, k3, k4, k5 = jax.random.split(key, 5)
        x = jax.random.normal(k1, (4, 512, H), dtype=jnp.float32)
        s_in = 1.0 / np.sqrt(H)
        Wqkv = jax.random.normal(k2, (H, 3 * D), dtype=jnp.float32) * s_in
        bqkv = jax.random.normal(k3, (3 * D,), dtype=jnp.float32) * 0.01
        Wo = jax.random.normal(k4, (D, H), dtype=jnp.float32) * (1.0 / np.sqrt(D))
        bo = jax.random.normal(k5, (H,), dtype=jnp.float32) * 0.01
        return {'x': x, 'Wqkv': Wqkv, 'bqkv': bqkv, 'Wo': Wo, 'bo': bo}
    _L1_attn_in = _L1_attn_setup()

    def _L1_ffn_setup():
        import jax, jax.numpy as jnp
        import numpy as np
        HIDDEN = 512
        INTER = 1376

        def _ternary_quantize(w):
            scale = jnp.mean(jnp.abs(w))
            return jnp.clip(jnp.round(w / scale), -1.0, 1.0) * scale
        key = jax.random.key(seed)
        kx, kg, ku, kd = jax.random.split(key, 4)
        x = jax.random.normal(kx, (2, 256, HIDDEN), dtype=jnp.float32)
        w_gate = _ternary_quantize(jax.random.normal(kg, (INTER, HIDDEN), dtype=jnp.float32) * 0.02)
        w_up = _ternary_quantize(jax.random.normal(ku, (INTER, HIDDEN), dtype=jnp.float32) * 0.02)
        w_down = _ternary_quantize(jax.random.normal(kd, (HIDDEN, INTER), dtype=jnp.float32) * 0.02)
        return {'x': x, 'w_gate': w_gate, 'w_up': w_up, 'w_down': w_down}
    _L1_ffn_in = _L1_ffn_setup()
    _d = {'L0_attn_data': _L0_attn_in['data'], 'L0_attn_weight': _L0_attn_in['weight'], 'L0_attn_mask': _L0_attn_in['mask'], 'L0_ffn_w_gate': _L0_ffn_in['w_gate'], 'L0_ffn_b_gate': _L0_ffn_in['b_gate'], 'L0_ffn_w_up': _L0_ffn_in['w_up'], 'L0_ffn_b_up': _L0_ffn_in['b_up'], 'L0_ffn_w_down': _L0_ffn_in['w_down'], 'L0_ffn_b_down': _L0_ffn_in['b_down'], 'L1_attn_Wqkv': _L1_attn_in['Wqkv'], 'L1_attn_bqkv': _L1_attn_in['bqkv'], 'L1_attn_Wo': _L1_attn_in['Wo'], 'L1_attn_bo': _L1_attn_in['bo'], 'L1_ffn_w_gate': _L1_ffn_in['w_gate'], 'L1_ffn_w_up': _L1_ffn_in['w_up'], 'L1_ffn_w_down': _L1_ffn_in['w_down']}
    _x0 = _d['L0_attn_data']
    _d['L0_attn_data'] = jax.random.normal(jax.random.fold_in(jax.random.key(seed), 1), (2, 512, 512), dtype=_x0.dtype)
    del _x0
    return _d

def reference(L0_attn_data, L0_attn_weight, L0_attn_mask, L0_ffn_w_gate, L0_ffn_b_gate, L0_ffn_w_up, L0_ffn_b_up, L0_ffn_w_down, L0_ffn_b_down, L1_attn_Wqkv, L1_attn_bqkv, L1_attn_Wo, L1_attn_bo, L1_ffn_w_gate, L1_ffn_w_up, L1_ffn_w_down):

    def _L0_attn_ref(data, weight, mask):
        import jax, jax.numpy as jnp
        import numpy as np
        BLOCK_H = 32
        BLOCK_W = 32
        N_FEAT = 512
        K_FEAT = 512
        N, K = weight.shape
        nb, kb = (N // BLOCK_H, K // BLOCK_W)
        block_mask = mask.reshape(nb, BLOCK_H, kb, BLOCK_W).astype(jnp.float32).sum(axis=(1, 3)) > 0
        elem_mask = jnp.repeat(jnp.repeat(block_mask, BLOCK_H, axis=0), BLOCK_W, axis=1)
        w_masked = weight * elem_mask.astype(weight.dtype)
        out = jnp.einsum('bsk,nk->bsn', data, w_masked)
        return out

    def _L0_ffn_ref(hidden_states, w_gate, b_gate, w_up, b_up, w_down, b_down):
        import jax, jax.numpy as jnp
        import numpy as np
        HIDDEN = 512
        INTER = 1376
        BATCH, SEQ = (2, 256)
        gate = jax.nn.silu(jnp.einsum('bsh,ih->bsi', hidden_states, w_gate) + b_gate)
        up = jnp.einsum('bsh,ih->bsi', hidden_states, w_up) + b_up
        return jnp.einsum('bsi,hi->bsh', gate * up, w_down) + b_down

    def _L1_attn_ref(x, Wqkv, bqkv, Wo, bo):
        import jax, jax.numpy as jnp
        import numpy as np
        H = 512
        D = H // 4
        B, S, C = x.shape
        d = C // 4
        qkv = jnp.einsum('bsc,cf->bsf', x, Wqkv) + bqkv
        qkv = qkv.reshape(B, S, 3, d)
        q, k, v = (qkv[:, :, 0], qkv[:, :, 1], qkv[:, :, 2])
        scale = 1.0 / jnp.sqrt(jnp.float32(d)).astype(x.dtype)
        attn = jnp.einsum('bqd,bkd->bqk', q, k) * scale
        attn = jax.nn.softmax(attn, axis=-1)
        out = jnp.einsum('bqk,bkd->bqd', attn, v)
        return jnp.einsum('bqd,dc->bqc', out, Wo) + bo

    def _L1_ffn_ref(x, w_gate, w_up, w_down):
        import jax, jax.numpy as jnp
        import numpy as np
        HIDDEN = 512
        INTER = 1376

        def _ternary_quantize(w):
            scale = jnp.mean(jnp.abs(w))
            return jnp.clip(jnp.round(w / scale), -1.0, 1.0) * scale
        xf = x.astype(jnp.float32) / 128.0
        gate = jnp.einsum('bsh,ih->bsi', xf, w_gate)
        up = jnp.einsum('bsh,ih->bsi', xf, w_up)
        inter = jax.nn.silu(gate) * up
        inter_q = jnp.trunc(jnp.clip(inter * 128.0, -128.0, 127.0)).astype(jnp.int8)
        down = jnp.einsum('bsi,hi->bsh', inter_q.astype(jnp.float32), w_down)
        out = jnp.trunc(jnp.clip(down * 128.0, -128.0, 127.0)).astype(jnp.int8)
        return out
    x = L0_attn_data
    x = x + _layernorm(_L0_attn_ref(_layernorm(x, axis=-1), L0_attn_weight, L0_attn_mask), axis=-1)
    x = x + _layernorm(_L0_ffn_ref(_layernorm(x, axis=-1), L0_ffn_w_gate, L0_ffn_b_gate, L0_ffn_w_up, L0_ffn_b_up, L0_ffn_w_down, L0_ffn_b_down), axis=-1)
    x = x + _layernorm(_L1_attn_ref(_layernorm(x, axis=-1), L1_attn_Wqkv, L1_attn_bqkv, L1_attn_Wo, L1_attn_bo), axis=-1)
    x = x + _layernorm(_L1_ffn_ref(_layernorm(x, axis=-1), L1_ffn_w_gate, L1_ffn_w_up, L1_ffn_w_down), axis=-1)
    return x

_drawn_inputs = setup_inputs


def setup_inputs(seed=0):
    import zlib

    import numpy as np

    out = dict(_drawn_inputs(seed))
    spreads = {}
    factors = {}
    for name, (base, spread) in spreads.items():
        noise = np.random.default_rng([zlib.crc32(name.encode()), seed]).standard_normal(out[name].shape)
        drawn = base * np.exp(spread * noise) if base else spread * noise
        out[name] = jnp.asarray(drawn.astype(out[name].dtype))
    for name, factor in factors.items():
        out[name] = (out[name] * factor).astype(out[name].dtype)
    return out
```

```python
from contextlib import ExitStack

import concourse.bass as bass
from concourse import mybir

P = 128
D = 512
KC = D // P
SEQ = 512
TT = SEQ // P
NSTREAM = 2
INTER = 1376
NI = -(-INTER // P)
BLK = 32
EPS = 1e-5
QSCALE = 128.0
ATT_SCALE = 1.0 / float(P) ** 0.5
NPASS = 2 * NSTREAM

ALU = mybir.AluOpType
ACT = mybir.ActivationFunctionType
F32 = mybir.dt.float32
F32R = mybir.dt.float32r
BF16 = mybir.dt.bfloat16
I16 = mybir.dt.int16
I32 = mybir.dt.int32
AX = mybir.AxisListType.X


def build_two_layers(nc, x_in, w_mix, mask, ffn_gu, ffn_d, b_gate, b_up, b_down, w_qkv, b_qk, b_v,
                     w_o, b_o, identity, block_ones, out):
    with ExitStack() as ctx:
        def sb(name, shape, dt=F32):
            return ctx.enter_context(nc.sbuf_tensor(name, shape, dt))

        def sem(name):
            return ctx.enter_context(nc.semaphore(name))

        x = sb("x", [P, NSTREAM * TT, D])
        xT_hi = sb("xT_hi", [P, NSTREAM, KC, SEQ], F32R)
        xT_lo = sb("xT_lo", [P, NSTREAM, KC, SEQ], F32R)
        raw_gu = sb("raw_gu", [P, 2, 2 * KC * P])
        raw_d = sb("raw_d", [P, 2, D])
        wgu_hi = sb("wgu_hi", [P, 2, 2, KC, P], F32R)
        wgu_lo = sb("wgu_lo", [P, 2, 2, KC, P], F32R)
        wd_hi = sb("wd_hi", [P, 2, D], F32R)
        wd_lo = sb("wd_lo", [P, 2, D], F32R)
        sil = sb("sil", [P, 2, SEQ])
        prod = sb("prod", [P, 2, SEQ])
        g_hi = sb("g_hi", [P, 2, SEQ], F32R)
        g_lo = sb("g_lo", [P, 2, SEQ], F32R)
        z = sb("z", [P, TT, D])
        y = sb("y", [P, 2, D])
        rnd = sb("rnd", [P, SEQ], I16)
        over = sb("over", [P, SEQ], BF16)
        near = sb("near", [P, SEQ], BF16)
        under = sb("under", [P, SEQ], BF16)
        stage = sb("stage", [P, KC, D])
        maskb = sb("maskb", [P, KC, D], I32)
        wide_hi = sb("wide_hi", [P, KC, D], F32R)
        wide_lo = sb("wide_lo", [P, KC, D], F32R)
        wqkv_hi = sb("wqkv_hi", [P, KC, 3 * P], F32R)
        wqkv_lo = sb("wqkv_lo", [P, KC, 3 * P], F32R)
        wo_hi = sb("wo_hi", [P, D], F32R)
        wo_lo = sb("wo_lo", [P, D], F32R)
        qkv = sb("qkv", [P, 3, SEQ])
        qkv_hi = sb("qkv_hi", [P, 3, SEQ], F32R)
        qkv_lo = sb("qkv_lo", [P, 3, SEQ], F32R)
        prob = sb("prob", [P, 2, SEQ])
        ident = sb("ident", [P, P])
        ones_blk = sb("ones_blk", [P, P])
        blk_rows = sb("blk_rows", [P, KC * D // BLK])
        keep = sb("keep", [P, KC, D // BLK])
        bg = sb("bg", [P, NI])
        bu = sb("bu", [P, NI])
        bd = sb("bd", [P, D])
        bqk = sb("bqk", [P, 2])
        bv = sb("bv", [P, P])
        bo = sb("bo", [P, D])
        stats = sb("stats", [P, 2, TT, 6])
        mv = sb("mv", [P, 2, TT, 2])
        var_eps = sb("var_eps", [P, 2, TT])
        rstd = sb("rstd", [P, 2, TT])
        neg_mr = sb("neg_mr", [P, TT])
        minus_half = sb("minus_half", [P, TT])
        row_max = sb("row_max", [P, 2])
        neg_max = sb("neg_max", [P, 2])
        row_sum = sb("row_sum", [P, 2])
        inv_sum = sb("inv_sum", [P, 2])

        acc = ctx.enter_context(nc.psum_tensor("acc", [P, TT, D], F32))
        ring = ctx.enter_context(nc.psum_tensor("ring", [P, 4, 512], F32))

        x_loaded = [sem(f"x_loaded{t}") for t in range(NSTREAM * TT)]
        mask_loaded, mix_loaded, const_loaded, bias_loaded, attw_loaded = map(
            sem, ["mask_loaded", "mix_loaded", "const_loaded", "bias_loaded", "attw_loaded"])
        gu_loaded = [sem(f"gu_loaded{i}") for i in range(2)]
        d_loaded = [sem(f"d_loaded{i}") for i in range(2)]
        stored = sem("stored")
        in_stats, in_aggr, in_var, in_rstd = map(sem, ["in_stats", "in_aggr", "in_var", "in_rstd"])
        y_ready, transposed, xT_hi_ready, xT_lo_ready = map(
            sem, ["y_ready", "transposed", "xT_hi_ready", "xT_lo_ready"])
        acc_ready, z_ready, z_step, out_stats, out_aggr, out_var, out_rstd, out_nmr, u_ready, x_updated = map(
            sem, ["acc_ready", "z_ready", "z_step", "out_stats", "out_aggr", "out_var", "out_rstd",
                  "out_nmr", "u_ready", "x_updated"])
        blk_summed, blk_spread, keep_ready, masked, mix_hi_ready, mix_lo_ready = map(
            sem, ["blk_summed", "blk_spread", "keep_ready", "masked", "mix_hi_ready", "mix_lo_ready"])
        wgu_hi_ready, wgu_lo_ready, wd_hi_ready, wd_lo_ready = map(
            sem, ["wgu_hi_ready", "wgu_lo_ready", "wd_hi_ready", "wd_lo_ready"])
        gate_ready, up_ready, down_done, silu_done, prod_ready, g_hi_ready, g_ready, trunc_step = map(
            sem, ["gate_ready", "up_ready", "down_done", "silu_done", "prod_ready", "g_hi_ready",
                  "g_ready", "trunc_step"])
        attw_hi_ready, attw_lo_ready = sem("attw_hi_ready"), sem("attw_lo_ready")
        qkv_prod, qkv_full, qkv_hi_ready, qkv_lo_ready = map(
            sem, ["qkv_prod", "qkv_full", "qkv_hi_ready", "qkv_lo_ready"])
        scored, maxed, max_scaled, exp_done, sum_inverted, prob_ready = map(
            sem, ["scored", "maxed", "max_scaled", "exp_done", "sum_inverted", "prob_ready"])
        prob_transposed, pT_hi_ready, pT_lo_ready = map(
            sem, ["prob_transposed", "pT_hi_ready", "pT_lo_ready"])
        mixed, oT_hi_ready, oT_lo_ready = map(sem, ["mixed", "oT_hi_ready", "oT_lo_ready"])
        half_set = sem("half_set")

        def f32(ap):
            return ap.bitcast(F32)

        def pass_bank(p):
            return (2 * NI * p) % 4

        def bank(r):
            return ring[:, r % 4, :]

        def tok(t):
            return slice(t * P, (t + 1) * P)

        def wait_down(eng, p, i, off=0):
            if i == 1 and p > 0:
                eng.wait_ge(acc_ready, 4 * (p + 1 if p <= NSTREAM else p + 3) + TT)
            elif i >= 2 or p > 0:
                eng.wait_ge(down_done, off + ((NI - 1) * p + max(i - 1, 0)))

        n_out = [1, 2, 5, 6]
        n_in = [3, 4, 7, None]
        block = ctx.enter_context(nc.Block())

        @block.sync
        def _(sp):
            for t in range(TT):
                sp.dma_start(x[:, t], x_in[t]).then_inc(x_loaded[t], 16)
            sp.dma_start(ident[:], identity).then_inc(const_loaded, 16)
            sp.dma_start(ones_blk[:], block_ones).then_inc(const_loaded, 16)
            sp.dma_start(maskb[:], mask).then_inc(mask_loaded, 16)
            sp.dma_start(stage[:], w_mix).then_inc(mix_loaded, 16)
            for t in range(TT, 2 * TT):
                sp.dma_start(x[:, t], x_in[t]).then_inc(x_loaded[t], 16)
            for i in range(2):
                sp.dma_start(raw_gu[:, i], ffn_gu[0, i]).then_inc(gu_loaded[i], 16)
                sp.dma_start(raw_d[:, i], ffn_d[0, i]).then_inc(d_loaded[i], 16)
            for dst, src in ((bg, b_gate), (bu, b_up), (bd, b_down), (bqk, b_qk), (bv, b_v), (bo, b_o)):
                sp.dma_start(dst[:], src).then_inc(bias_loaded, 16)
            sp.wait_ge(masked, KC)
            sp.dma_start(stage[:, 0:3].rearrange("p a b -> p (a b)"), w_qkv).then_inc(attw_loaded, 16)
            sp.dma_start(stage[:, 3], w_o).then_inc(attw_loaded, 16)

            def load_gu(layer, i, g, par):
                sp.wait_ge(wgu_lo_ready, g - 1)
                sp.dma_start(raw_gu[:, par], ffn_gu[layer, i]).then_inc(gu_loaded[par], 16)

            def load_d(layer, i, g, par):
                sp.wait_ge(wd_lo_ready, g - 1)
                sp.dma_start(raw_d[:, par], ffn_d[layer, i]).then_inc(d_loaded[par], 16)

            for p in range(NPASS):
                g0, layer = NI * p, p // NSTREAM

                def load(i):
                    if p > 0 or i >= 2:
                        load_d(layer, i, g0 + i, (g0 + i) % 2)
                    if i + 2 < NI:
                        load_gu(layer, i + 2, g0 + i + 2, (g0 + i) % 2)
                    elif p + 1 < NPASS:
                        load_gu((p + 1) // NSTREAM, i + 2 - NI, g0 + i + 2, (g0 + i) % 2)

                load(0)
                load(1)
                with sp.Fori(0, (NI - 5) // 2) as j:
                    for i in (2, 3):
                        load_d(layer, 2 * j + i, 2 * j + (g0 + i), (g0 + i) % 2)
                        load_gu(layer, 2 * j + (i + 2), 2 * j + (g0 + i + 2), (g0 + i) % 2)
                for i in range(NI - 3, NI):
                    load(i)
            for t in range(NSTREAM * TT):
                sp.wait_ge(x_updated, 3 * NSTREAM * TT + t + 1)
                sp.dma_start(out[t], x[:, t]).then_inc(stored, 16)
            sp.wait_ge(stored, 16 * NSTREAM * TT)

        @block.gpsimd
        def _(pool):
            nc.gpsimd.memset(minus_half[:], -0.5).then_inc(half_set, 1)
            pool.wait_ge(half_set, 1)

            def before(n):
                pool.wait_ge(in_var, n + 1)
                nc.gpsimd.tensor_tensor(rstd[:, 0], var_eps[:, 0], minus_half[:], ALU.pow).then_inc(in_rstd, 1)

            def after(n):
                pool.wait_ge(out_var, n + 1)
                nc.gpsimd.tensor_tensor(rstd[:, 1], var_eps[:, 1], minus_half[:], ALU.pow).then_inc(out_rstd, 1)

            before(0)
            before(1)
            for n in range(2, 8):
                after(n - 2)
                before(n)
            after(6)
            after(7)

        @block.scalar
        def _(act):
            def split_gu_hi(g, par):
                act.wait_ge(gu_loaded[par], (g // 2 + 1) * 16 if isinstance(g, int) else g * 8 + (16 - 8 * par))
                src = raw_gu[:, par].rearrange("p (a b) -> p a b", a=2)
                nc.scalar.copy(wgu_hi[:, par].rearrange("p a k m -> p a (k m)"), src).then_inc(wgu_hi_ready, 1)

            def split_d_hi(g, par):
                act.wait_ge(d_loaded[par], (g // 2 + 1) * 16 if isinstance(g, int) else g * 8 + (16 - 8 * par))
                nc.scalar.copy(wd_hi[:, par], raw_d[:, par]).then_inc(wd_hi_ready, 1)

            def xT_hi_tiles(n, r):
                s = n % 2
                for t in range(TT):
                    act.wait_ge(transposed, 4 * n + t + 1)
                    nc.scalar.copy(xT_hi[:, s, :, tok(t)],
                                   bank(r + t).rearrange("p (k m) -> p k m", k=KC)).then_inc(xT_hi_ready, 1)

            def normalise(n):
                act.wait_ge(out_nmr, n + 1)
                for t in range(TT):
                    nc.scalar.activation(z[:, t], z[:, t], ACT.Identity, bias=neg_mr[:, t:t + 1],
                                         scale=rstd[:, 1, t:t + 1]).then_inc(u_ready, 1)

            def tile(p, i, par, b, first=False, ahead=True, j=None):
                layer, down_wait = p // NSTREAM, (p, i, 0 if j is None else 2 * j)
                g = NI * p + i
                if j is not None:
                    i, g = 2 * j + i, 2 * j + g
                act.wait_ge(gate_ready, g + 1)
                if not first:
                    act.wait_ge(prod_ready, g - 1)
                if layer == 0:
                    nc.scalar.activation(sil[:, par], bank(b), ACT.Silu, bias=bg[:, bass.ds(i, 1)]).then_inc(silu_done, 1)
                else:
                    nc.scalar.activation(sil[:, par], bank(b), ACT.Silu, scale=1.0 / QSCALE).then_inc(silu_done, 1)
                if ahead:
                    act.wait_ge(up_ready, g + 1)
                    split_gu_hi(g + 2, par)
                wait_down(act, *down_wait)
                if layer == 0:
                    act.wait_ge(prod_ready, g + 1)
                    nc.scalar.copy(g_hi[:, par], prod[:, par]).then_inc(g_hi_ready, 1)
                split_d_hi(g, par)

            def ffn(p):
                g0, layer, last = NI * p, p // NSTREAM, p == NPASS - 1
                r0 = pass_bank(p)
                tile(p, 0, g0 % 2, r0, first=p == 0)
                if n_out[p] is not None:
                    normalise(n_out[p])
                for i in (1, 2):
                    tile(p, i, (g0 + i) % 2, r0 + 2 * i, first=p == 0 and i < 2)
                if p == 0:
                    act.wait_ge(attw_loaded, 32)
                    nc.scalar.copy(wqkv_hi[:].rearrange("p k m -> p (k m)"),
                                   stage[:, 0:3].rearrange("p a b -> p (a b)")).then_inc(attw_hi_ready, 1)
                    nc.scalar.copy(wo_hi[:], stage[:, 3]).then_inc(attw_hi_ready, 1)
                with act.Fori(0, (NI - 3) // 2 - last) as j:
                    for h in (3, 4):
                        tile(p, h, (g0 + h) % 2, r0 + 2 * h, j=j)
                if last:
                    for i in (NI - 2, NI - 1):
                        tile(p, i, (g0 + i) % 2, r0 + 2 * i, ahead=False)
                if n_in[p] is not None:
                    xT_hi_tiles(n_in[p], r0 + 2 * NI)

            def attention(s):
                r, n = pass_bank(2), 4 + s
                act.wait_ge(bias_loaded, 16 * 6)
                for a in range(2):
                    act.wait_ge(qkv_prod, 3 * s + a + 1)
                    if s:
                        act.wait_ge(qkv_lo_ready, 3 * s)
                    nc.scalar.activation(qkv[:, a], bank(r + a), ACT.Identity, bias=bqk[:, a:a + 1]).then_inc(qkv_full, 1)
                normalise(3 + s)
                for t in range(TT):
                    m = 4 * s + t
                    act.wait_ge(max_scaled, m + 1)
                    if m >= 2:
                        act.wait_ge(prob_transposed, m - 1)
                    nc.scalar.activation(prob[:, m % 2], bank(r + 3 + t), ACT.Exp, bias=neg_max[:, m % 2:m % 2 + 1],
                                         scale=ATT_SCALE, accum_out=row_sum[:, m % 2:m % 2 + 1]).then_inc(exp_done, 1)
                    if t >= 1:
                        pT_hi(m - 1, t - 1, r)
                pT_hi(4 * s + TT - 1, TT - 1, r)
                act.wait_ge(mixed, s + 1)
                nc.scalar.copy(qkv_hi[:, 0], bank(r + 11)).then_inc(oT_hi_ready, 1)

            def pT_hi(m, t, r):
                act.wait_ge(prob_transposed, m + 1)
                nc.scalar.copy(wide_hi[:, :, tok(t)],
                               bank(r + 7 + t).rearrange("p (k m) -> p k m", k=KC)).then_inc(pT_hi_ready, 1)

            xT_hi_tiles(0, 0)
            for k in range(KC):
                act.wait_ge(masked, k + 1)
                nc.scalar.copy(wide_hi[:, k], f32(maskb[:, k])).then_inc(mix_hi_ready, 1)
            xT_hi_tiles(1, 0)
            for g in range(2):
                split_gu_hi(g, g)
            normalise(0)
            xT_hi_tiles(2, 0)
            act.wait_ge(bias_loaded, 16 * 6)
            ffn(0)
            ffn(1)
            attention(0)
            xT_hi_tiles(5, pass_bank(2))
            attention(1)
            xT_hi_tiles(6, pass_bank(2))
            ffn(2)
            ffn(3)
            normalise(7)

        @block.vector
        def _(dve):
            V = nc.vector

            def stats_before(n):
                s = n % 2
                for t in range(TT):
                    if n < 2:
                        dve.wait_ge(x_loaded[4 * s + t], 16)
                    else:
                        dve.wait_ge(x_updated, 4 * (n - 2) + t + 1)
                    V.bn_stats(stats[:, 0, t], x[:, 4 * s + t]).then_inc(in_stats, 1)
                for t in range(TT):
                    dve.wait_ge(in_stats, 4 * n + t + 1)
                    V.bn_aggr(mv[:, 0, t], stats[:, 0, t]).then_inc(in_aggr, 1)
                dve.wait_ge(in_aggr, 4 * n + TT)
                V.tensor_scalar(var_eps[:, 0], mv[:, 0, :, 1], EPS, None, ALU.add).then_inc(in_var, 1)

            def transpose_before(n, r):
                s = n % 2

                def low(t):
                    dve.wait_ge(xT_hi_ready, 4 * n + t + 1)
                    V.tensor_tensor(xT_lo[:, s, :, tok(t)], bank(r + t).rearrange("p (k m) -> p k m", k=KC),
                                    f32(xT_hi[:, s, :, tok(t)]), ALU.subtract).then_inc(xT_lo_ready, 1)

                dve.wait_ge(in_rstd, n + 1)
                for t in range(TT):
                    m = 4 * n + t
                    if m >= 2:
                        dve.wait_ge(transposed, m - 1)
                    V.tensor_scalar(y[:, m % 2], x[:, 4 * s + t], mv[:, 0, t, 0:1], rstd[:, 0, t:t + 1],
                                    ALU.subtract, ALU.mult).then_inc(y_ready, 1)
                    if t >= 1:
                        low(t - 1)
                low(TT - 1)

            def truncate(src, dst, count, done, dst_free=None):
                V.tensor_scalar(rnd[:], src, -128.0, 127.0, ALU.max, ALU.min).then_inc(trunc_step, 1)
                dve.wait_ge(trunc_step, count + 1)
                V.scalar_tensor_tensor(out=over[:], in0=src, scalar=0.0, in1=rnd[:], op0=ALU.max,
                                       op1=ALU.is_lt).then_inc(trunc_step, 1)
                V.scalar_tensor_tensor(out=under[:], in0=src, scalar=0.0, in1=rnd[:], op0=ALU.min,
                                       op1=ALU.is_gt).then_inc(trunc_step, 1)
                dve.wait_ge(trunc_step, count + 2)
                V.tensor_tensor(near[:], rnd[:], over[:], ALU.subtract).then_inc(trunc_step, 1)
                dve.wait_ge(trunc_step, count + 4)
                if dst_free is not None:
                    dst_free()
                V.tensor_tensor(dst, near[:], under[:], ALU.add).then_inc(done, 1)

            def evacuate(n):
                kind = n // 2
                for t in range(TT):
                    dve.wait_ge(acc_ready, 4 * n + t + 1)
                    if kind in (1, 2):
                        V.tensor_tensor(z[:, t], acc[:, t], (bd if kind == 1 else bo)[:], ALU.add).then_inc(z_ready, 1)
                    elif kind == 0:
                        V.tensor_copy(z[:, t], acc[:, t]).then_inc(z_ready, 1)
                    else:
                        V.tensor_scalar(z[:, t], acc[:, t], QSCALE, None, ALU.mult).then_inc(z_step, 1)
                        dve.wait_ge(z_step, 4 * (n - 6) + t + 1)
                        truncate(z[:, t], z[:, t], trunc_count(n, t), z_ready)
                for t in range(TT):
                    dve.wait_ge(z_ready, 4 * n + t + 1)
                    V.bn_stats(stats[:, 1, t], z[:, t]).then_inc(out_stats, 1)
                for t in range(TT):
                    dve.wait_ge(out_stats, 4 * n + t + 1)
                    V.bn_aggr(mv[:, 1, t], stats[:, 1, t]).then_inc(out_aggr, 1)
                dve.wait_ge(out_aggr, 4 * n + TT)
                V.tensor_scalar(var_eps[:, 1], mv[:, 1, :, 1], EPS, None, ALU.add).then_inc(out_var, 1)

            def shift_after(n):
                dve.wait_ge(out_rstd, n + 1)
                V.scalar_tensor_tensor(out=neg_mr[:], in0=mv[:, 1, :, 0], scalar=-1.0, in1=rstd[:, 1],
                                       op0=ALU.mult, op1=ALU.mult).then_inc(out_nmr, 1)

            def residual(n):
                s = n % 2
                for t in range(TT):
                    dve.wait_ge(u_ready, 4 * n + t + 1)
                    V.tensor_tensor(x[:, 4 * s + t], x[:, 4 * s + t], z[:, t], ALU.add).then_inc(x_updated, 1)

            def trunc_count(n, t):
                done = 4 * (NI + TT * 0) if n == 6 else 4 * (2 * NI + TT)
                return done + 4 * t

            def split_gu_lo(g, par):
                dve.wait_ge(wgu_hi_ready, g + 1)
                V.tensor_tensor(wgu_lo[:, par].rearrange("p a k m -> p (a k m)"), raw_gu[:, par],
                                f32(wgu_hi[:, par].rearrange("p a k m -> p (a k m)")),
                                ALU.subtract).then_inc(wgu_lo_ready, 1)

            def tile(p, i, par, b, first=False, ahead=True, truncs=0, j=None):
                layer, down_wait = p // NSTREAM, (p, i, 0 if j is None else 2 * j)
                g = NI * p + i
                if j is not None:
                    i, g = 2 * j + i, 2 * j + g
                dve.wait_ge(silu_done, g + 1)
                dve.wait_ge(up_ready, g + 1)
                if layer == 0:
                    if not first:
                        dve.wait_ge(g_ready, g - 1)
                    V.scalar_tensor_tensor(out=prod[:, par], in0=bank(b + 1), scalar=bu[:, bass.ds(i, 1)],
                                           in1=sil[:, par], op0=ALU.add, op1=ALU.mult).then_inc(prod_ready, 1)
                else:
                    dve.wait_ge(g_ready, g - 1)
                    V.tensor_tensor(prod[:, par], bank(b + 1), sil[:, par], ALU.mult).then_inc(prod_ready, 1)
                if ahead:
                    split_gu_lo(g + 2, par)
                if layer == 0:
                    dve.wait_ge(g_hi_ready, g + 1)
                    V.tensor_tensor(g_lo[:, par], prod[:, par], f32(g_hi[:, par]), ALU.subtract).then_inc(g_ready, 1)
                else:
                    dve.wait_ge(prod_ready, g + 1)
                    truncate(prod[:, par], g_hi[:, par], truncs, g_ready,
                             lambda: wait_down(dve, *down_wait))
                dve.wait_ge(wd_hi_ready, g + 1)
                V.tensor_tensor(wd_lo[:, par], raw_d[:, par], f32(wd_hi[:, par]), ALU.subtract).then_inc(wd_lo_ready, 1)

            def ffn(p):
                g0, layer, last = NI * p, p // NSTREAM, p == NPASS - 1
                r0 = pass_bank(p)
                t0 = {2: 0, 3: 4 * (NI + TT)}.get(p, 0)
                if n_out[p] is not None:
                    evacuate(n_out[p])
                tile(p, 0, g0 % 2, r0, first=p == 0, truncs=t0)
                if n_out[p] is not None:
                    shift_after(n_out[p])
                tile(p, 1, (g0 + 1) % 2, r0 + 2, first=p == 0, truncs=t0 + 4)
                if n_out[p] is not None:
                    residual(n_out[p])
                    if n_in[p] is not None:
                        stats_before(n_in[p])
                tile(p, 2, g0 % 2, r0 + 4, truncs=t0 + 8)
                if p == 0:
                    dve.wait_ge(attw_hi_ready, 1)
                    V.tensor_tensor(wqkv_lo[:].rearrange("p k m -> p (k m)"), stage[:, 0:3].rearrange("p a b -> p (a b)"),
                                    f32(wqkv_hi[:].rearrange("p k m -> p (k m)")), ALU.subtract).then_inc(attw_lo_ready, 1)
                    dve.wait_ge(attw_hi_ready, 2)
                    V.tensor_tensor(wo_lo[:], stage[:, 3], f32(wo_hi[:]), ALU.subtract).then_inc(attw_lo_ready, 1)
                with dve.Fori(0, (NI - 3) // 2 - last) as j:
                    for h in (3, 4):
                        tile(p, h, (g0 + h) % 2, r0 + 2 * h, truncs=8 * j + (t0 + 4 * h), j=j)
                if last:
                    for i in (NI - 2, NI - 1):
                        tile(p, i, (g0 + i) % 2, r0 + 2 * i, ahead=False, truncs=t0 + 4 * i)
                if n_in[p] is not None:
                    transpose_before(n_in[p], r0 + 2 * NI)

            def attention(s):
                r = pass_bank(2)

                def split(a):
                    dve.wait_ge(qkv_full, 3 * s + a + 1)
                    V.tensor_copy(qkv_hi[:, a], qkv[:, a]).then_inc(qkv_hi_ready, 1)
                    dve.wait_ge(qkv_hi_ready, 3 * s + a + 1)
                    V.tensor_tensor(qkv_lo[:, a], qkv[:, a], f32(qkv_hi[:, a]), ALU.subtract).then_inc(qkv_lo_ready, 1)

                split(0)
                split(1)
                dve.wait_ge(qkv_prod, 3 * s + 3)
                V.tensor_tensor(qkv[:, 2].rearrange("p (t d) -> p t d", t=TT),
                                bank(r + 2).rearrange("p (t d) -> p t d", t=TT),
                                bv[:].unsqueeze(1).broadcast_to([P, TT, P]), ALU.add).then_inc(qkv_full, 1)
                split(2)

                def softmax_max(t):
                    m = 4 * s + t
                    q = slice(m % 2, m % 2 + 1)
                    dve.wait_ge(scored, m + 1)
                    V.reduce_max(row_max[:, q], bank(r + 3 + t), AX).then_inc(maxed, 1)
                    dve.wait_ge(maxed, m + 1)
                    if m >= 2:
                        dve.wait_ge(exp_done, m - 1)
                    V.tensor_scalar(neg_max[:, q], row_max[:, q], -ATT_SCALE, None, ALU.mult).then_inc(max_scaled, 1)

                def softmax_scale(t):
                    m = 4 * s + t
                    q = slice(m % 2, m % 2 + 1)
                    dve.wait_ge(exp_done, m + 1)
                    V.reciprocal(inv_sum[:, q], row_sum[:, q]).then_inc(sum_inverted, 1)
                    dve.wait_ge(sum_inverted, m + 1)
                    V.tensor_scalar(prob[:, m % 2], prob[:, m % 2], inv_sum[:, q], None, ALU.mult).then_inc(prob_ready, 1)

                def prob_low(t):
                    dve.wait_ge(pT_hi_ready, 4 * s + t + 1)
                    V.tensor_tensor(wide_lo[:, :, tok(t)], bank(r + 7 + t).rearrange("p (k m) -> p k m", k=KC),
                                    f32(wide_hi[:, :, tok(t)]), ALU.subtract).then_inc(pT_lo_ready, 1)

                softmax_max(0)
                for t in range(TT):
                    if t + 1 < TT:
                        softmax_max(t + 1)
                    softmax_scale(t)
                    if t >= 1:
                        prob_low(t - 1)
                prob_low(TT - 1)
                dve.wait_ge(oT_hi_ready, s + 1)
                V.tensor_tensor(qkv_lo[:, 0], bank(r + 11), f32(qkv_hi[:, 0]), ALU.subtract).then_inc(oT_lo_ready, 1)

            stats_before(0)
            dve.wait_ge(mask_loaded, 16)
            V.reduce_sum(blk_rows[:], maskb[:].rearrange("p k (b c) -> p (k b) c", c=BLK), AX).then_inc(blk_summed, 1)
            transpose_before(0, 0)
            dve.wait_ge(blk_spread, 1)
            V.tensor_scalar(keep[:].rearrange("p k b -> p (k b)"), ring[:, 0, 0:KC * D // BLK], 0.0, None,
                            ALU.is_gt).then_inc(keep_ready, 1)
            dve.wait_ge(keep_ready, 1)
            dve.wait_ge(mix_loaded, 16)
            for k in range(KC):
                V.tensor_tensor(f32(maskb[:, k]).rearrange("p (b c) -> p b c", c=BLK),
                                stage[:, k].rearrange("p (b c) -> p b c", c=BLK),
                                keep[:, k].unsqueeze(2).broadcast_to([P, D // BLK, BLK]),
                                ALU.mult).then_inc(masked, 1)
            for k in range(KC):
                dve.wait_ge(mix_hi_ready, k + 1)
                V.tensor_tensor(wide_lo[:, k], f32(maskb[:, k]), f32(wide_hi[:, k]), ALU.subtract).then_inc(mix_lo_ready, 1)
            stats_before(1)
            transpose_before(1, 0)
            for g in range(2):
                split_gu_lo(g, g)
            dve.wait_ge(bias_loaded, 16 * 6)
            evacuate(0)
            shift_after(0)
            residual(0)
            stats_before(2)
            transpose_before(2, 0)
            ffn(0)
            ffn(1)
            evacuate(3)
            shift_after(3)
            attention(0)
            residual(3)
            stats_before(5)
            transpose_before(5, pass_bank(2))
            evacuate(4)
            shift_after(4)
            attention(1)
            residual(4)
            stats_before(6)
            transpose_before(6, pass_bank(2))
            ffn(2)
            ffn(3)
            evacuate(7)
            shift_after(7)
            residual(7)

        @block.tensor
        def _(pe):
            def product(dst, w, m, start, stop):
                terms = [(a, b) for a, b in ((w[0], m[0]), (w[0], m[1]), (w[1], m[0])) if a is not None and b is not None]
                for q, (a, b) in enumerate(terms):
                    ins = nc.tensor.matmul(dst, a, b, start=start and q == 0, stop=stop and q == len(terms) - 1)
                return ins

            def transposes(n, r, free=None):
                for t in range(TT):
                    m = 4 * n + t
                    pe.wait_ge(y_ready, m + 1)
                    if free:
                        free(t)
                    for k in range(KC):
                        ins = nc.tensor.transpose(bank(r + t)[:, tok(k)], y[:, m % 2, tok(k)], ident[:])
                    ins.then_inc(transposed, 1)

            def linear(n, w_hi, w_lo):
                s = n % 2
                pe.wait_ge(xT_lo_ready, 4 * n + TT)
                for t in range(TT):
                    if n >= 1:
                        pe.wait_ge(z_ready, 4 * (n - 1) + t + 1)
                    for k in range(KC):
                        ins = product(acc[:, t], (xT_hi[:, s, k, tok(t)], xT_lo[:, s, k, tok(t)]),
                                      (w_hi[:, k], w_lo[:, k]), k == 0, k == KC - 1)
                    ins.then_inc(acc_ready, 1)

            def gate_up(s, g, par, b, ring_used=True):
                pe.wait_ge(wgu_lo_ready, g + 1)
                for a, (used, ready) in enumerate(((silu_done, gate_ready), (prod_ready, up_ready))):
                    if ring_used:
                        pe.wait_ge(used, g - 1)
                    for k in range(KC):
                        ins = product(bank(b + a), (wgu_hi[:, par, a, k], wgu_lo[:, par, a, k]),
                                      (xT_hi[:, s, k], xT_lo[:, s, k]), k == 0, k == KC - 1)
                    ins.then_inc(ready, 1)

            def down(layer, n, g, par, start=False, stop=False):
                pe.wait_ge(g_ready, g + 1)
                pe.wait_ge(wd_lo_ready, g + 1)
                for t in range(TT):
                    if start:
                        pe.wait_ge(z_ready, 4 * (n - 1) + t + 1)
                    low = g_lo[:, par, tok(t)] if layer == 0 else None
                    ins = product(acc[:, t], (g_hi[:, par, tok(t)], low), (wd_hi[:, par], wd_lo[:, par]), start, stop)
                    if stop:
                        ins.then_inc(acc_ready, 1)
                if not stop:
                    ins.then_inc(down_done, 1)

            def ffn(p):
                s, g0, layer = p % NSTREAM, NI * p, p // NSTREAM
                n = (2 if layer == 0 else 6) + s
                r0 = pass_bank(p)

                def gu(i, j=0, used=True):
                    gate_up(s, 2 * j + (g0 + i) if not isinstance(j, int) else g0 + i, (g0 + i) % 2, r0 + 2 * i, used)

                def dn(i, j=0, **kw):
                    down(layer, n, 2 * j + (g0 + i) if not isinstance(j, int) else g0 + i, (g0 + i) % 2, **kw)

                pe.wait_ge(xT_lo_ready, 4 * n + TT)
                gu(0, used=False)
                gu(1, used=False)
                gu(2)
                dn(0, start=True)
                with pe.Fori(0, (NI - 3) // 2) as j:
                    for h in range(2):
                        gu(3 + h, j)
                        dn(1 + h, j)
                dn(NI - 2)
                if n_in[p] is not None:
                    def free(t):
                        g = g0 + NI - 2 + t // 2
                        pe.wait_ge(silu_done if t % 2 == 0 else prod_ready, g + 1)
                    transposes(n_in[p], r0 + 2 * NI, free)
                dn(NI - 1, stop=True)

            def attention(s):
                r, n = pass_bank(2), 4 + s
                pe.wait_ge(xT_lo_ready, 4 * n + TT)
                pe.wait_ge(attw_lo_ready, 2)
                for a in range(2):
                    for k in range(KC):
                        ins = product(bank(r + a), (wqkv_hi[:, k, tok(a)], wqkv_lo[:, k, tok(a)]),
                                      (xT_hi[:, s, k], xT_lo[:, s, k]), k == 0, k == KC - 1)
                    ins.then_inc(qkv_prod, 1)
                for t in range(TT):
                    for k in range(KC):
                        ins = product(bank(r + 2)[:, tok(t)], (xT_hi[:, s, k, tok(t)], xT_lo[:, s, k, tok(t)]),
                                      (wqkv_hi[:, k, tok(2)], wqkv_lo[:, k, tok(2)]), k == 0, k == KC - 1)
                ins.then_inc(qkv_prod, 1)
                pe.wait_ge(qkv_lo_ready, 3 * s + 2)
                for t in range(TT):
                    if t == 3:
                        pe.wait_ge(qkv_full, 3 * s + 3)
                    ins = product(bank(r + 3 + t), (qkv_hi[:, 0, tok(t)], qkv_lo[:, 0, tok(t)]),
                                  (qkv_hi[:, 1], qkv_lo[:, 1]), True, True)
                    ins.then_inc(scored, 1)
                for t in range(TT):
                    m = 4 * s + t
                    pe.wait_ge(prob_ready, m + 1)
                    for k in range(KC):
                        ins = nc.tensor.transpose(bank(r + 7 + t)[:, tok(k)], prob[:, m % 2, tok(k)], ident[:])
                    ins.then_inc(prob_transposed, 1)
                pe.wait_ge(pT_lo_ready, 4 * s + TT)
                pe.wait_ge(qkv_lo_ready, 3 * s + 3)
                for k in range(KC):
                    ins = product(bank(r + 11), (qkv_hi[:, 2, tok(k)], qkv_lo[:, 2, tok(k)]),
                                  (wide_hi[:, k], wide_lo[:, k]), k == 0, k == KC - 1)
                ins.then_inc(mixed, 1)
                pe.wait_ge(oT_lo_ready, s + 1)
                for t in range(TT):
                    pe.wait_ge(z_ready, 4 * (n - 1) + t + 1)
                    product(acc[:, t], (qkv_hi[:, 0, tok(t)], qkv_lo[:, 0, tok(t)]),
                            (wo_hi[:], wo_lo[:]), True, True).then_inc(acc_ready, 1)

            pe.wait_ge(const_loaded, 32)
            transposes(0, 0)
            pe.wait_ge(blk_summed, 1)
            pe.wait_ge(xT_lo_ready, 1)
            nc.tensor.matmul(ring[:, 0, 0:KC * D // BLK], ones_blk[:], blk_rows[:], start=True, stop=True).then_inc(blk_spread, 1)
            pe.wait_ge(mix_lo_ready, KC)
            linear(0, wide_hi, wide_lo)
            pe.wait_ge(keep_ready, 1)
            transposes(1, 0)
            linear(1, wide_hi, wide_lo)
            pe.wait_ge(xT_lo_ready, 8)
            transposes(2, 0)
            ffn(0)
            ffn(1)
            attention(0)
            transposes(5, pass_bank(2))
            attention(1)
            transposes(6, pass_bank(2))
            ffn(2)
            ffn(3)


def kernel(L0_attn_data, L0_attn_weight, L0_attn_mask, L0_ffn_w_gate, L0_ffn_b_gate, L0_ffn_w_up, L0_ffn_b_up,
           L0_ffn_w_down, L0_ffn_b_down, L1_attn_Wqkv, L1_attn_bqkv, L1_attn_Wo, L1_attn_bo, L1_ffn_w_gate,
           L1_ffn_w_up, L1_ffn_w_down):
    import numpy as np
    import concourse.bacc as bacc
    from concourse.bass_utils import run_bass_kernel_spmd

    def chunked(w):
        return np.asarray(w).reshape(KC, P, -1).transpose(1, 0, 2)

    def padded(w):
        w = np.asarray(w)
        return np.concatenate([w, np.zeros((NI * P - INTER,) + w.shape[1:], w.dtype)])

    def by_feature(w):
        return padded(w).reshape(NI, P, KC, P).transpose(0, 3, 2, 1)

    def columns(b):
        return padded(b).reshape(NI, P).T

    def rows(b):
        b = np.asarray(b)
        return np.broadcast_to(b, (P, b.size))

    bqkv = np.asarray(L1_attn_bqkv)
    gu = np.stack([np.stack([by_feature(a), by_feature(b)], axis=2)
                   for a, b in ((L0_ffn_w_gate, L0_ffn_w_up), (L1_ffn_w_gate, L1_ffn_w_up))])
    arrays = {
        "x_in": np.asarray(L0_attn_data).reshape(NSTREAM * TT, P, D),
        "w_mix": chunked(np.asarray(L0_attn_weight).T),
        "mask": chunked(np.asarray(L0_attn_mask).T),
        "ffn_gu": gu.reshape(2, NI, P, 2 * KC * P),
        "ffn_d": np.stack([padded(np.asarray(w).T).reshape(NI, P, D) for w in (L0_ffn_w_down, L1_ffn_w_down)]),
        "b_gate": columns(L0_ffn_b_gate),
        "b_up": columns(L0_ffn_b_up),
        "b_down": rows(L0_ffn_b_down),
        "w_qkv": chunked(L1_attn_Wqkv).reshape(P, KC * 3 * P),
        "b_qk": bqkv[:2 * P].reshape(2, P).T,
        "b_v": rows(bqkv[2 * P:]),
        "w_o": np.asarray(L1_attn_Wo),
        "b_o": rows(L1_attn_bo),
        "identity": np.eye(P, dtype=np.float32),
        "block_ones": np.kron(np.eye(P // BLK, dtype=np.float32), np.ones((BLK, BLK), np.float32)),
    }
    arrays = {f"{k}_dram": np.ascontiguousarray(a) for k, a in arrays.items()}
    nc = bacc.Bacc("TRN2", target_bir_lowering=False, num_devices=1)
    args = [nc.dram_tensor(k, a.shape, mybir.dt.from_np(a.dtype), kind="ExternalInput").ap()
            for k, a in arrays.items()]
    args.append(nc.dram_tensor("out_dram", (NSTREAM * TT, P, D), F32, kind="ExternalOutput").ap())
    build_two_layers(nc, *args)
    r = run_bass_kernel_spmd(nc, [arrays], core_ids=[0])
    return r.results[0]["out_dram"].reshape(NSTREAM, SEQ, D)
```

```python
from contextlib import ExitStack

import concourse.bass as bass
from concourse import mybir

P = 128
D = 512
KC = D // P
SEQ = 512
TT = SEQ // P
NSTREAM = 2
INTER = 1376
NI = -(-INTER // P)
BLK = 32
EPS = 1e-5
QSCALE = 128.0
ATT_SCALE = 1.0 / float(P) ** 0.5
NPASS = 2 * NSTREAM

ALU = mybir.AluOpType
ACT = mybir.ActivationFunctionType
F32 = mybir.dt.float32
F32R = mybir.dt.float32r
BF16 = mybir.dt.bfloat16
I16 = mybir.dt.int16
I32 = mybir.dt.int32
AX = mybir.AxisListType.X


def build_two_layers(nc, x_in, w_mix, mask, ffn_gu, ffn_d, b_gate, b_up, b_down, w_qkv, b_qk, b_v,
                     w_o, b_o, identity, block_ones, out):
    with ExitStack() as ctx:
        def sb(name, shape, dt=F32):
            return ctx.enter_context(nc.sbuf_tensor(name, shape, dt))

        def sem(name):
            return ctx.enter_context(nc.semaphore(name))

        x = sb("x", [P, NSTREAM * TT, D])
        xT_hi = sb("xT_hi", [P, NSTREAM, KC, SEQ], F32R)
        xT_lo = sb("xT_lo", [P, NSTREAM, KC, SEQ], F32R)
        raw_gu = sb("raw_gu", [P, 2, 2 * KC * P])
        raw_d = sb("raw_d", [P, 2, D])
        wgu_hi = sb("wgu_hi", [P, 2, 2, KC, P], F32R)
        wgu_lo = sb("wgu_lo", [P, 2, 2, KC, P], F32R)
        wd_hi = sb("wd_hi", [P, 2, D], F32R)
        wd_lo = sb("wd_lo", [P, 2, D], F32R)
        sil = sb("sil", [P, 2, SEQ])
        prod = sb("prod", [P, 2, SEQ])
        g_hi = sb("g_hi", [P, 2, SEQ], F32R)
        g_lo = sb("g_lo", [P, 2, SEQ], F32R)
        z = sb("z", [P, TT, D])
        y = sb("y", [P, TT, D])
        mag = sb("mag", [P, SEQ])
        sgn = sb("sgn", [P, SEQ], BF16)
        rnd = sb("rnd", [P, SEQ], I16)
        over = sb("over", [P, SEQ], BF16)
        floor = sb("floor", [P, SEQ], BF16)
        signed = sb("signed", [P, SEQ], BF16)
        stage = sb("stage", [P, KC, D])
        maskb = sb("maskb", [P, KC, D], I32)
        wide_hi = sb("wide_hi", [P, KC, D], F32R)
        wide_lo = sb("wide_lo", [P, KC, D], F32R)
        wqkv_hi = sb("wqkv_hi", [P, KC, 3 * P], F32R)
        wqkv_lo = sb("wqkv_lo", [P, KC, 3 * P], F32R)
        wo_hi = sb("wo_hi", [P, D], F32R)
        wo_lo = sb("wo_lo", [P, D], F32R)
        qkv = sb("qkv", [P, 3, SEQ])
        qkv_hi = sb("qkv_hi", [P, 3, SEQ], F32R)
        qkv_lo = sb("qkv_lo", [P, 3, SEQ], F32R)
        prob = sb("prob", [P, 2, SEQ])
        out_mag = y
        out_sgn = prob[:].rearrange("p a b -> p (a b)").bitcast(BF16).rearrange("p (t b) -> p t b", t=TT)
        ident = sb("ident", [P, P])
        ones_blk = sb("ones_blk", [P, P])
        blk_rows = sb("blk_rows", [P, KC * D // BLK])
        keep = sb("keep", [P, KC, D // BLK])
        bg = sb("bg", [P, NI])
        bu = sb("bu", [P, NI])
        bd = sb("bd", [P, D])
        bqk = sb("bqk", [P, 2])
        bv = sb("bv", [P, P])
        bo = sb("bo", [P, D])
        stats = sb("stats", [P, 2, TT, 6])
        mv = sb("mv", [P, 2, TT, 2])
        var_eps = sb("var_eps", [P, 2, TT])
        rstd = sb("rstd", [P, 2, TT])
        neg_mr = sb("neg_mr", [P, TT])
        minus_half = sb("minus_half", [P, TT])
        row_max = sb("row_max", [P, 2])
        neg_max = sb("neg_max", [P, 2])
        row_sum = sb("row_sum", [P, 2])
        inv_sum = sb("inv_sum", [P, 2])

        acc = ctx.enter_context(nc.psum_tensor("acc", [P, TT, D], F32))
        ring = ctx.enter_context(nc.psum_tensor("ring", [P, 4, 512], F32))

        x_loaded = [sem(f"x_loaded{t}") for t in range(NSTREAM * TT)]
        mask_loaded, mix_loaded, const_loaded, bias_loaded, attw_loaded = map(
            sem, ["mask_loaded", "mix_loaded", "const_loaded", "bias_loaded", "attw_loaded"])
        gu_loaded = [sem(f"gu_loaded{i}") for i in range(2)]
        d_loaded = [sem(f"d_loaded{i}") for i in range(2)]
        stored = sem("stored")
        in_stats, in_aggr, in_var, in_rstd = map(sem, ["in_stats", "in_aggr", "in_var", "in_rstd"])
        y_ready, transposed, xT_hi_ready, xT_lo_ready = map(
            sem, ["y_ready", "transposed", "xT_hi_ready", "xT_lo_ready"])
        acc_ready, z_ready, mag_ready, sgn_ready, out_mag_ready, out_sgn_ready, out_stats, out_aggr, out_var, out_rstd, out_nmr, u_ready, x_updated = map(
            sem, ["acc_ready", "z_ready", "mag_ready", "sgn_ready", "out_mag_ready", "out_sgn_ready", "out_stats", "out_aggr", "out_var", "out_rstd",
                  "out_nmr", "u_ready", "x_updated"])
        blk_summed, blk_spread, keep_ready, mix_hi_ready, mix_lo_ready = map(
            sem, ["blk_summed", "blk_spread", "keep_ready", "mix_hi_ready", "mix_lo_ready"])
        masked = [sem(f"masked{k}") for k in range(KC)]
        wgu_hi_ready, wgu_lo_ready, wd_hi_ready, wd_lo_ready = map(
            sem, ["wgu_hi_ready", "wgu_lo_ready", "wd_hi_ready", "wd_lo_ready"])
        gate_ready, up_ready, down_done, silu_done, prod_ready, g_hi_ready, g_ready, trunc_step = map(
            sem, ["gate_ready", "up_ready", "down_done", "silu_done", "prod_ready", "g_hi_ready",
                  "g_ready", "trunc_step"])
        attw_hi_ready, attw_lo_ready = sem("attw_hi_ready"), sem("attw_lo_ready")
        qk_prod, qk_full, qk_hi_ready, qk_lo_ready = map(sem, ["qk_prod", "qk_full", "qk_hi_ready", "qk_lo_ready"])
        v_prod, v_full, v_hi_ready, v_lo_ready = map(sem, ["v_prod", "v_full", "v_hi_ready", "v_lo_ready"])
        scored, maxed, max_scaled, exp_done, sum_inverted, prob_ready = map(
            sem, ["scored", "maxed", "max_scaled", "exp_done", "sum_inverted", "prob_ready"])
        prob_transposed, pT_hi_ready, pT_lo_ready = map(
            sem, ["prob_transposed", "pT_hi_ready", "pT_lo_ready"])
        mixed, oT_hi_ready, oT_lo_ready = map(sem, ["mixed", "oT_hi_ready", "oT_lo_ready"])
        half_set = sem("half_set")

        def f32(ap):
            return ap.bitcast(F32)

        def pass_bank(p):
            return (2 * NI * p) % 4

        def bank(r):
            return ring[:, r % 4, :]

        def tok(t):
            return slice(t * P, (t + 1) * P)

        def wait_acc_free(eng, n, t):
            if 1 <= n <= 2:
                eng.wait_ge(u_ready, 4 * (n - 1) + t + 1)
            elif 3 <= n <= 6:
                eng.wait_ge(z_ready, 4 * (n - 3) + t + 1)
            elif n == 7:
                eng.wait_ge(out_mag_ready, t + 1)

        def mask_weights(eng, k):
            return eng.tensor_tensor(f32(maskb[:, k]).rearrange("p (b c) -> p b c", c=BLK),
                                     stage[:, k].rearrange("p (b c) -> p b c", c=BLK),
                                     keep[:, k].unsqueeze(2).broadcast_to([P, D // BLK, BLK]), ALU.mult)

        def wait_down(eng, p, i, off=0):
            if i == 1 and p > 0:
                eng.wait_ge(acc_ready, 4 * (p + 1 if p <= NSTREAM else p + 3) + TT)
            elif i >= 2 or p > 0:
                eng.wait_ge(down_done, off + ((NI - 1) * p + max(i - 1, 0)))

        n_out = [1, 2, 5, 6]
        n_in = [3, 4, 7, None]
        block = ctx.enter_context(nc.Block())

        @block.sync
        def _(sp):
            for t in range(TT):
                sp.dma_start(x[:, t], x_in[t]).then_inc(x_loaded[t], 16)
            sp.dma_start(ident[:], identity).then_inc(const_loaded, 16)
            sp.dma_start(ones_blk[:], block_ones).then_inc(const_loaded, 16)
            sp.dma_start(maskb[:], mask).then_inc(mask_loaded, 16)
            sp.dma_start(stage[:], w_mix).then_inc(mix_loaded, 16)
            for t in range(TT, 2 * TT):
                sp.dma_start(x[:, t], x_in[t]).then_inc(x_loaded[t], 16)
            for i in range(2):
                sp.dma_start(raw_gu[:, i], ffn_gu[0, i]).then_inc(gu_loaded[i], 16)
                sp.dma_start(raw_d[:, i], ffn_d[0, i]).then_inc(d_loaded[i], 16)
            for dst, src in ((bg, b_gate), (bu, b_up), (bd, b_down), (bqk, b_qk), (bv, b_v), (bo, b_o)):
                sp.dma_start(dst[:], src).then_inc(bias_loaded, 16)
            for k in range(KC):
                sp.wait_ge(masked[k], 1)
            sp.dma_start(stage[:, 0:3].rearrange("p a b -> p (a b)"), w_qkv).then_inc(attw_loaded, 16)
            sp.dma_start(stage[:, 3], w_o).then_inc(attw_loaded, 16)

            def load_gu(layer, i, g, par):
                sp.wait_ge(wgu_lo_ready, g - 1)
                sp.dma_start(raw_gu[:, par], ffn_gu[layer, i]).then_inc(gu_loaded[par], 16)

            def load_d(layer, i, g, par):
                sp.wait_ge(wd_lo_ready, g - 1)
                sp.dma_start(raw_d[:, par], ffn_d[layer, i]).then_inc(d_loaded[par], 16)

            for p in range(NPASS):
                g0, layer = NI * p, p // NSTREAM

                def load(i):
                    if p > 0 or i >= 2:
                        load_d(layer, i, g0 + i, (g0 + i) % 2)
                    if i + 2 < NI:
                        load_gu(layer, i + 2, g0 + i + 2, (g0 + i) % 2)
                    elif p + 1 < NPASS:
                        load_gu((p + 1) // NSTREAM, i + 2 - NI, g0 + i + 2, (g0 + i) % 2)

                load(0)
                load(1)
                with sp.Fori(0, (NI - 5) // 2) as j:
                    for i in (2, 3):
                        load_d(layer, 2 * j + i, 2 * j + (g0 + i), (g0 + i) % 2)
                        load_gu(layer, 2 * j + (i + 2), 2 * j + (g0 + i + 2), (g0 + i) % 2)
                for i in range(NI - 3, NI):
                    load(i)
            for t in range(NSTREAM * TT):
                sp.wait_ge(x_updated, 3 * NSTREAM * TT + t + 1)
                sp.dma_start(out[t], x[:, t]).then_inc(stored, 16)
            sp.wait_ge(stored, 16 * NSTREAM * TT)

        @block.gpsimd
        def _(pool):
            G = nc.gpsimd
            G.memset(minus_half[:], -0.5).then_inc(half_set, 1)
            pool.wait_ge(half_set, 1)

            def before(n):
                pool.wait_ge(in_var, n + 1)
                G.tensor_tensor(rstd[:, 0], var_eps[:, 0], minus_half[:], ALU.pow).then_inc(in_rstd, 1)

            def after(n):
                pool.wait_ge(out_var, n + 1)
                G.tensor_tensor(rstd[:, 1], var_eps[:, 1], minus_half[:], ALU.pow).then_inc(out_rstd, 1)

            def split_gu_lo(g, par):
                pool.wait_ge(wgu_hi_ready, g + 1)
                G.tensor_tensor(wgu_lo[:, par].rearrange("p a k m -> p (a k m)"), raw_gu[:, par],
                                f32(wgu_hi[:, par].rearrange("p a k m -> p (a k m)")),
                                ALU.subtract).then_inc(wgu_lo_ready, 1)

            def split_d_lo(g, par):
                pool.wait_ge(wd_hi_ready, g + 1)
                G.tensor_tensor(wd_lo[:, par], raw_d[:, par], f32(wd_hi[:, par]), ALU.subtract).then_inc(wd_lo_ready, 1)

            def tile(g, par, ahead=True):
                if ahead:
                    split_gu_lo(g + 2, par)
                split_d_lo(g, par)

            def ffn(p):
                g0, last = NI * p, p == NPASS - 1
                if not last:
                    after(n_out[p])
                for i in range(3):
                    tile(g0 + i, (g0 + i) % 2)
                    if i == 1 and not last:
                        before(n_in[p])
                if last:
                    after(n_out[p])
                if p == 0:
                    pool.wait_ge(attw_hi_ready, 1)
                    G.tensor_tensor(wqkv_lo[:].rearrange("p k m -> p (k m)"), stage[:, 0:3].rearrange("p a b -> p (a b)"),
                                    f32(wqkv_hi[:].rearrange("p k m -> p (k m)")), ALU.subtract).then_inc(attw_lo_ready, 1)
                    pool.wait_ge(attw_hi_ready, 2)
                    G.tensor_tensor(wo_lo[:], stage[:, 3], f32(wo_hi[:]), ALU.subtract).then_inc(attw_lo_ready, 1)
                with pool.Fori(0, (NI - 3) // 2 - last) as j:
                    for h in (3, 4):
                        tile(2 * j + (g0 + h), (g0 + h) % 2)
                if last:
                    for i in (NI - 2, NI - 1):
                        tile(g0 + i, (g0 + i) % 2, ahead=False)

            def attention(s):
                n = 3 + s
                after(n)
                for t in range(TT):
                    pool.wait_ge(u_ready, 4 * n + t + 1)
                    x_t = x[:, 4 * (n % 2) + t]
                    G.tensor_tensor(x_t, x_t, z[:, t], ALU.add).then_inc(x_updated, 1)
                before(n + 2)

            before(0)
            for k in range(KC // 2, KC):
                pool.wait_ge(keep_ready, 1)
                pool.wait_ge(mix_loaded, 16)
                mask_weights(G, k).then_inc(masked[k], 1)
            before(1)
            for g in range(2):
                split_gu_lo(g, g)
            after(0)
            before(2)
            ffn(0)
            ffn(1)
            attention(0)
            attention(1)
            ffn(2)
            ffn(3)
            for t in range(TT):
                pool.wait_ge(out_var, 8 + t)
                G.tensor_tensor(rstd[:, 1, t:t + 1], var_eps[:, 1, t:t + 1], minus_half[:, 0:1], ALU.pow).then_inc(out_rstd, 1)

        @block.scalar
        def _(act):
            def split_gu_hi(g, par):
                act.wait_ge(gu_loaded[par], (g // 2 + 1) * 16 if isinstance(g, int) else g * 8 + (16 - 8 * par))
                src = raw_gu[:, par].rearrange("p (a b) -> p a b", a=2)
                nc.scalar.copy(wgu_hi[:, par].rearrange("p a k m -> p a (k m)"), src).then_inc(wgu_hi_ready, 1)

            def split_d_hi(g, par):
                act.wait_ge(d_loaded[par], (g // 2 + 1) * 16 if isinstance(g, int) else g * 8 + (16 - 8 * par))
                nc.scalar.copy(wd_hi[:, par], raw_d[:, par]).then_inc(wd_hi_ready, 1)

            def xT_hi_tiles(n, r):
                s = n % 2
                for t in range(TT):
                    act.wait_ge(transposed, 4 * n + t + 1)
                    nc.scalar.copy(xT_hi[:, s, :, tok(t)],
                                   bank(r + t).rearrange("p (k m) -> p k m", k=KC)).then_inc(xT_hi_ready, 1)

            def normalise(n, tiles=range(TT)):
                for t in tiles:
                    act.wait_ge(out_nmr, n + 1 + (t if n == 7 else 0))
                    src = acc if n < 2 else z
                    if n < 2 and n > 0:
                        act.wait_ge(x_updated, 4 * (n - 1) + t + 1)
                    nc.scalar.activation(z[:, t], src[:, t], ACT.Identity, bias=neg_mr[:, t:t + 1],
                                         scale=rstd[:, 1, t:t + 1]).then_inc(u_ready, 1)

            def magnitudes(n, tiles=range(TT)):
                for t in tiles:
                    act.wait_ge(acc_ready, 4 * n + t + 1)
                    if n == 6:
                        act.wait_ge(transposed, 4 * 8)
                    else:
                        act.wait_ge(z_ready, 4 * (6 - 2) + t + 1)
                    nc.scalar.activation(out_sgn[:, t], acc[:, t], ACT.Sign).then_inc(out_sgn_ready, 1)
                    nc.scalar.activation(out_mag[:, t], acc[:, t], ACT.Abs, scale=QSCALE).then_inc(out_mag_ready, 1)

            def tile(p, i, par, b, first=False, ahead=True, j=None):
                layer, down_wait = p // NSTREAM, (p, i, 0 if j is None else 2 * j)
                g = NI * p + i
                if j is not None:
                    i, g = 2 * j + i, 2 * j + g
                act.wait_ge(gate_ready, g + 1)
                if not first:
                    act.wait_ge(prod_ready, g - 1)
                if layer == 0:
                    nc.scalar.activation(sil[:, par], bank(b), ACT.Silu, bias=bg[:, bass.ds(i, 1)]).then_inc(silu_done, 1)
                else:
                    nc.scalar.activation(sil[:, par], bank(b), ACT.Silu, scale=1.0 / QSCALE).then_inc(silu_done, 1)
                if ahead:
                    act.wait_ge(up_ready, g + 1)
                    split_gu_hi(g + 2, par)
                wait_down(act, *down_wait)
                if layer == 0:
                    act.wait_ge(prod_ready, g + 1)
                    nc.scalar.copy(g_hi[:, par], prod[:, par]).then_inc(g_hi_ready, 1)
                else:
                    act.wait_ge(prod_ready, g + 1)
                    act.wait_ge(g_ready, g)
                    nc.scalar.activation(mag[:], prod[:, par], ACT.Abs).then_inc(mag_ready, 1)
                    nc.scalar.activation(sgn[:], prod[:, par], ACT.Sign).then_inc(sgn_ready, 1)
                split_d_hi(g, par)

            def ffn(p):
                g0, layer, last = NI * p, p // NSTREAM, p == NPASS - 1
                r0 = pass_bank(p)
                if last:
                    magnitudes(6)
                tile(p, 0, g0 % 2, r0, first=p == 0)
                if not last:
                    normalise(n_out[p])
                for i in (1, 2):
                    tile(p, i, (g0 + i) % 2, r0 + 2 * i, first=p == 0 and i < 2)
                if last:
                    normalise(6)
                if p == 0:
                    act.wait_ge(attw_loaded, 32)
                    nc.scalar.copy(wqkv_hi[:].rearrange("p k m -> p (k m)"),
                                   stage[:, 0:3].rearrange("p a b -> p (a b)")).then_inc(attw_hi_ready, 1)
                    nc.scalar.copy(wo_hi[:], stage[:, 3]).then_inc(attw_hi_ready, 1)
                with act.Fori(0, (NI - 3) // 2 - last) as j:
                    for h in (3, 4):
                        tile(p, h, (g0 + h) % 2, r0 + 2 * h, j=j)
                if last:
                    for i in (NI - 2, NI - 1):
                        tile(p, i, (g0 + i) % 2, r0 + 2 * i, ahead=False)
                if n_in[p] is not None:
                    xT_hi_tiles(n_in[p], r0 + 2 * NI)

            def attention(s):
                r = pass_bank(2)
                for q, a in enumerate((1, 0)):
                    act.wait_ge(qk_prod, 2 * s + q + 1)
                    if s:
                        act.wait_ge(qk_lo_ready, 2)
                    nc.scalar.activation(qkv[:, a], bank(r + q), ACT.Identity, bias=bqk[:, a:a + 1]).then_inc(qk_full, 1)
                    act.wait_ge(qk_full, 2 * s + q + 1)
                    nc.scalar.copy(qkv_hi[:, a], qkv[:, a]).then_inc(qk_hi_ready, 1)

                def exp(t):
                    m = 4 * s + t
                    act.wait_ge(max_scaled, m + 1)
                    if m >= 2:
                        act.wait_ge(prob_transposed, m - 1)
                    nc.scalar.activation(prob[:, m % 2], acc[:, t], ACT.Exp, bias=neg_max[:, m % 2:m % 2 + 1],
                                         scale=ATT_SCALE, accum_out=row_sum[:, m % 2:m % 2 + 1]).then_inc(exp_done, 1)

                def pT_hi(t):
                    act.wait_ge(prob_transposed, 4 * s + t + 1)
                    nc.scalar.copy(wide_hi[:, :, tok(t)],
                                   bank(r + 3 + t).rearrange("p (k m) -> p k m", k=KC)).then_inc(pT_hi_ready, 1)

                def oT_hi(h):
                    act.wait_ge(mixed, 2 * s + h + 1)
                    c = slice(h * SEQ // 2, (h + 1) * SEQ // 2)
                    nc.scalar.copy(qkv_hi[:, 0, c], bank(r + 3)[:, c]).then_inc(oT_hi_ready, 1)

                normalise(3 + s, (0, 1))
                exp(0)
                exp(1)
                normalise(3 + s, (2, 3))
                pT_hi(0)
                exp(2)
                act.wait_ge(v_full, s + 1)
                nc.scalar.copy(qkv_hi[:, 2], qkv[:, 2]).then_inc(v_hi_ready, 1)
                pT_hi(1)
                exp(3)
                pT_hi(2)
                oT_hi(0)
                pT_hi(3)
                oT_hi(1)
                xT_hi_tiles(5 + s, r)

            xT_hi_tiles(0, 0)
            for k in range(KC):
                act.wait_ge(masked[k], 1)
                nc.scalar.copy(wide_hi[:, k], f32(maskb[:, k])).then_inc(mix_hi_ready, 1)
            xT_hi_tiles(1, 0)
            for g in range(2):
                split_gu_hi(g, g)
            normalise(0)
            xT_hi_tiles(2, 0)
            act.wait_ge(bias_loaded, 16 * 6)
            ffn(0)
            ffn(1)
            attention(0)
            attention(1)
            ffn(2)
            ffn(3)
            magnitudes(7)
            normalise(7)

        @block.vector
        def _(dve):
            V = nc.vector

            def stats_before(n):
                s = n % 2
                for t in range(TT):
                    if n < 2:
                        dve.wait_ge(x_loaded[4 * s + t], 16)
                    else:
                        dve.wait_ge(x_updated, 4 * (n - 2) + t + 1)
                    V.bn_stats(stats[:, 0, t], x[:, 4 * s + t]).then_inc(in_stats, 1)
                for t in range(TT):
                    dve.wait_ge(in_stats, 4 * n + t + 1)
                    V.bn_aggr(mv[:, 0, t], stats[:, 0, t]).then_inc(in_aggr, 1)
                dve.wait_ge(in_aggr, 4 * n + TT)
                V.tensor_scalar(var_eps[:, 0], mv[:, 0, :, 1], EPS, None, ALU.add).then_inc(in_var, 1)

            def scale_before(n):
                dve.wait_ge(in_rstd, n + 1)
                for t in range(TT):
                    if n >= 1:
                        dve.wait_ge(transposed, 4 * (n - 1) + t + 1)
                    V.tensor_scalar(y[:, t], x[:, 4 * (n % 2) + t], mv[:, 0, t, 0:1], rstd[:, 0, t:t + 1],
                                    ALU.subtract, ALU.mult).then_inc(y_ready, 1)

            def xT_low(n, r):
                s = n % 2
                for t in range(TT):
                    dve.wait_ge(xT_hi_ready, 4 * n + t + 1)
                    V.tensor_tensor(xT_lo[:, s, :, tok(t)], bank(r + t).rearrange("p (k m) -> p k m", k=KC),
                                    f32(xT_hi[:, s, :, tok(t)]), ALU.subtract).then_inc(xT_lo_ready, 1)

            def truncate(mag_ap, sgn_ap, dst, count, done, wait_sgn, dst_free=None):
                V.tensor_scalar(rnd[:], mag_ap, 128.0, None, ALU.min).then_inc(trunc_step, 1)
                dve.wait_ge(trunc_step, count + 1)
                V.tensor_tensor(over[:], mag_ap, rnd[:], ALU.is_lt).then_inc(trunc_step, 1)
                dve.wait_ge(trunc_step, count + 2)
                V.tensor_tensor(floor[:], rnd[:], over[:], ALU.subtract).then_inc(trunc_step, 1)
                dve.wait_ge(trunc_step, count + 3)
                wait_sgn()
                V.tensor_tensor(signed[:], floor[:], sgn_ap, ALU.mult).then_inc(trunc_step, 1)
                dve.wait_ge(trunc_step, count + 4)
                if dst_free is not None:
                    dst_free()
                V.tensor_scalar(dst, signed[:], 127.0, None, ALU.min).then_inc(done, 1)

            def truncate_result(n, t):
                dve.wait_ge(out_mag_ready, 4 * (n - 6) + t + 1)
                if n == 7:
                    dve.wait_ge(x_updated, 4 * 6 + t + 1)
                truncate(out_mag[:, t], out_sgn[:, t], z[:, t], trunc_count(n, t), z_ready,
                         lambda: dve.wait_ge(out_sgn_ready, 4 * (n - 6) + t + 1))

            def result_stats(n, t):
                if n >= 2:
                    dve.wait_ge(z_ready, 4 * (n - 2) + t + 1)
                    src = z
                else:
                    dve.wait_ge(acc_ready, 4 * n + t + 1)
                    src = acc
                V.bn_stats(stats[:, 1, t], src[:, t]).then_inc(out_stats, 1)
                return src

            def variances(n):
                for t in range(TT):
                    dve.wait_ge(out_stats, 4 * n + t + 1)
                    V.bn_aggr(mv[:, 1, t], stats[:, 1, t]).then_inc(out_aggr, 1)
                dve.wait_ge(out_aggr, 4 * n + TT)
                V.tensor_scalar(var_eps[:, 1], mv[:, 1, :, 1], EPS, None, ALU.add).then_inc(out_var, 1)

            def evacuate(n):
                if n >= 2:
                    for t in range(TT):
                        dve.wait_ge(acc_ready, 4 * n + t + 1)
                        V.tensor_tensor(z[:, t], acc[:, t], (bd if n < 4 else bo)[:], ALU.add).then_inc(z_ready, 1)
                for t in range(TT):
                    result_stats(n, t)
                variances(n)

            def shift_after(n):
                dve.wait_ge(out_rstd, n + 1)
                V.scalar_tensor_tensor(out=neg_mr[:], in0=mv[:, 1, :, 0], scalar=-1.0, in1=rstd[:, 1],
                                       op0=ALU.mult, op1=ALU.mult).then_inc(out_nmr, 1)

            def shift_last(t):
                dve.wait_ge(out_rstd, 8 + t)
                V.scalar_tensor_tensor(out=neg_mr[:, t:t + 1], in0=mv[:, 1, t, 0:1], scalar=-1.0, in1=rstd[:, 1, t:t + 1],
                                       op0=ALU.mult, op1=ALU.mult).then_inc(out_nmr, 1)

            def residual(n, tiles=range(TT)):
                s = n % 2
                for t in tiles:
                    dve.wait_ge(u_ready, 4 * n + t + 1)
                    V.tensor_tensor(x[:, 4 * s + t], x[:, 4 * s + t], z[:, t], ALU.add).then_inc(x_updated, 1)

            def trunc_count(n, t):
                if n == 7:
                    return 4 * (2 * NI + TT + t)
                return 4 * (NI + t + (1 if t >= 2 else 0))

            def pass_trunc_count(p, i):
                if p == 2:
                    return 4 * i
                return 4 * (NI + i + (TT if i >= 1 else 2))

            def tile(p, i, par, b, first=False, truncs=0, j=None):
                layer, down_wait = p // NSTREAM, (p, i, 0 if j is None else 2 * j)
                g = NI * p + i
                if j is not None:
                    i, g = 2 * j + i, 2 * j + g
                dve.wait_ge(silu_done, g + 1)
                dve.wait_ge(up_ready, g + 1)
                if layer == 0:
                    if not first:
                        dve.wait_ge(g_ready, g - 1)
                    V.scalar_tensor_tensor(out=prod[:, par], in0=bank(b + 1), scalar=bu[:, bass.ds(i, 1)],
                                           in1=sil[:, par], op0=ALU.add, op1=ALU.mult).then_inc(prod_ready, 1)
                else:
                    dve.wait_ge(g_ready, g - 1)
                    V.tensor_tensor(prod[:, par], bank(b + 1), sil[:, par], ALU.mult).then_inc(prod_ready, 1)
                if layer == 0:
                    dve.wait_ge(g_hi_ready, g + 1)
                    V.tensor_tensor(g_lo[:, par], prod[:, par], f32(g_hi[:, par]), ALU.subtract).then_inc(g_ready, 1)
                else:
                    dve.wait_ge(mag_ready, g - (NSTREAM * NI - 1))
                    truncate(mag[:], sgn[:], g_hi[:, par], truncs, g_ready,
                             lambda: dve.wait_ge(sgn_ready, g - (NSTREAM * NI - 1)),
                             lambda: wait_down(dve, *down_wait))

            def ffn(p):
                g0, last = NI * p, p == NPASS - 1
                r0 = pass_bank(p)

                def one(i):
                    tile(p, i, (g0 + i) % 2, r0 + 2 * i, first=p == 0 and i < 2,
                         truncs=pass_trunc_count(p, i) if p >= 2 else 0)

                if last:
                    truncate_result(6, 0)
                    truncate_result(6, 1)
                    one(0)
                    truncate_result(6, 2)
                    truncate_result(6, 3)
                    one(1)
                    for t in range(TT):
                        result_stats(6, t)
                    variances(6)
                    one(2)
                    shift_after(6)
                else:
                    evacuate(n_out[p])
                    one(0)
                    shift_after(n_out[p])
                    one(1)
                    residual(n_out[p])
                    stats_before(n_in[p])
                    one(2)
                    scale_before(n_in[p])
                with dve.Fori(0, (NI - 3) // 2 - last) as j:
                    for h in (3, 4):
                        tile(p, h, (g0 + h) % 2, r0 + 2 * h,
                             truncs=8 * j + pass_trunc_count(p, h) if p >= 2 else 0, j=j)
                if last:
                    residual(6)
                    one(NI - 2)
                    one(NI - 1)
                else:
                    xT_low(n_in[p], r0 + 2 * NI)

            def attention(s):
                r, c = pass_bank(2), 3 + s

                def softmax_max(t):
                    m = 4 * s + t
                    q = slice(m % 2, m % 2 + 1)
                    dve.wait_ge(scored, m + 1)
                    V.reduce_max(row_max[:, q], acc[:, t], AX).then_inc(maxed, 1)
                    dve.wait_ge(maxed, m + 1)
                    if m >= 2:
                        dve.wait_ge(exp_done, m - 1)
                    V.tensor_scalar(neg_max[:, q], row_max[:, q], -ATT_SCALE, None, ALU.mult).then_inc(max_scaled, 1)

                def softmax_scale(t):
                    m = 4 * s + t
                    q = slice(m % 2, m % 2 + 1)
                    dve.wait_ge(exp_done, m + 1)
                    V.reciprocal(inv_sum[:, q], row_sum[:, q]).then_inc(sum_inverted, 1)
                    dve.wait_ge(sum_inverted, m + 1)
                    V.tensor_scalar(prob[:, m % 2], prob[:, m % 2], inv_sum[:, q], None, ALU.mult).then_inc(prob_ready, 1)

                def pT_low(t):
                    dve.wait_ge(pT_hi_ready, 4 * s + t + 1)
                    V.tensor_tensor(wide_lo[:, :, tok(t)], bank(r + 3 + t).rearrange("p (k m) -> p k m", k=KC),
                                    f32(wide_hi[:, :, tok(t)]), ALU.subtract).then_inc(pT_lo_ready, 1)

                def oT_low(h):
                    dve.wait_ge(oT_hi_ready, 2 * s + h + 1)
                    q = slice(h * SEQ // 2, (h + 1) * SEQ // 2)
                    V.tensor_tensor(qkv_lo[:, 0, q], bank(r + 3)[:, q], f32(qkv_hi[:, 0, q]),
                                    ALU.subtract).then_inc(oT_lo_ready, 1)

                evacuate(c)
                for q, a in enumerate((1, 0)):
                    dve.wait_ge(qk_hi_ready, 2 * s + q + 1)
                    V.tensor_tensor(qkv_lo[:, a], qkv[:, a], f32(qkv_hi[:, a]), ALU.subtract).then_inc(qk_lo_ready, 1)
                shift_after(c)
                softmax_max(0)
                softmax_max(1)
                softmax_scale(0)
                dve.wait_ge(v_prod, s + 1)
                V.tensor_tensor(qkv[:, 2].rearrange("p (t d) -> p t d", t=TT),
                                bank(r + 2).rearrange("p (t d) -> p t d", t=TT),
                                bv[:].unsqueeze(1).broadcast_to([P, TT, P]), ALU.add).then_inc(v_full, 1)
                softmax_max(2)
                softmax_scale(1)
                pT_low(0)
                softmax_max(3)
                softmax_scale(2)
                dve.wait_ge(v_hi_ready, s + 1)
                V.tensor_tensor(qkv_lo[:, 2], qkv[:, 2], f32(qkv_hi[:, 2]), ALU.subtract).then_inc(v_lo_ready, 1)
                pT_low(1)
                softmax_scale(3)
                pT_low(2)
                stats_before(c + 2)
                oT_low(0)
                pT_low(3)
                scale_before(c + 2)
                oT_low(1)
                xT_low(c + 2, r)

            stats_before(0)
            scale_before(0)
            dve.wait_ge(mask_loaded, 16)
            V.reduce_sum(blk_rows[:], maskb[:].rearrange("p k (b c) -> p (k b) c", c=BLK), AX).then_inc(blk_summed, 1)
            dve.wait_ge(blk_spread, 1)
            V.tensor_scalar(keep[:].rearrange("p k b -> p (k b)"), acc[:, 0, 0:KC * D // BLK], 0.0, None,
                            ALU.is_gt).then_inc(keep_ready, 1)
            dve.wait_ge(keep_ready, 1)
            dve.wait_ge(mix_loaded, 16)
            for k in range(KC // 2):
                mask_weights(V, k).then_inc(masked[k], 1)
            xT_low(0, 0)
            for k in range(KC):
                dve.wait_ge(mix_hi_ready, k + 1)
                V.tensor_tensor(wide_lo[:, k], f32(maskb[:, k]), f32(wide_hi[:, k]), ALU.subtract).then_inc(mix_lo_ready, 1)
            stats_before(1)
            scale_before(1)
            xT_low(1, 0)
            evacuate(0)
            shift_after(0)
            residual(0)
            stats_before(2)
            scale_before(2)
            xT_low(2, 0)
            dve.wait_ge(bias_loaded, 16 * 6)
            ffn(0)
            ffn(1)
            attention(0)
            attention(1)
            ffn(2)
            ffn(3)
            for t in range(TT):
                truncate_result(7, t)
                result_stats(7, t)
                dve.wait_ge(out_stats, 4 * 7 + t + 1)
                V.bn_aggr(mv[:, 1, t], stats[:, 1, t]).then_inc(out_aggr, 1)
                dve.wait_ge(out_aggr, 4 * 7 + t + 1)
                V.tensor_scalar(var_eps[:, 1, t:t + 1], mv[:, 1, t, 1:2], EPS, None, ALU.add).then_inc(out_var, 1)
                if t >= 1:
                    shift_last(t - 1)
                if t >= 2:
                    residual(7, (t - 2,))
            shift_last(TT - 1)
            residual(7, (TT - 2, TT - 1))

        @block.tensor
        def _(pe):
            def product(dst, w, m, start, stop):
                terms = [(a, b) for a, b in ((w[0], m[0]), (w[0], m[1]), (w[1], m[0])) if a is not None and b is not None]
                for q, (a, b) in enumerate(terms):
                    ins = nc.tensor.matmul(dst, a, b, start=start and q == 0, stop=stop and q == len(terms) - 1)
                return ins

            def transposes(n, r, free=None):
                for t in range(TT):
                    m = 4 * n + t
                    pe.wait_ge(y_ready, m + 1)
                    if free:
                        free(t)
                    for k in range(KC):
                        ins = nc.tensor.transpose(bank(r + t)[:, tok(k)], y[:, t, tok(k)], ident[:])
                    ins.then_inc(transposed, 1)

            def linear(n, w_hi, w_lo, before_last=None):
                s = n % 2
                for k in range(KC):
                    if n == 0:
                        pe.wait_ge(mix_lo_ready, k + 1)
                    if k == KC - 1 and before_last is not None:
                        before_last()
                    for t in range(TT):
                        if k == 0:
                            pe.wait_ge(xT_lo_ready, 4 * n + t + 1)
                            wait_acc_free(pe, n, t)
                        ins = product(acc[:, t], (xT_hi[:, s, k, tok(t)], xT_lo[:, s, k, tok(t)]),
                                      (w_hi[:, k], w_lo[:, k]), k == 0, k == KC - 1)
                        if k == KC - 1:
                            ins.then_inc(acc_ready, 1)

            def gate_up(s, g, par, b, ring_used=True):
                pe.wait_ge(wgu_lo_ready, g + 1)
                for a, (used, ready) in enumerate(((silu_done, gate_ready), (prod_ready, up_ready))):
                    if ring_used:
                        pe.wait_ge(used, g - 1)
                    for k in range(KC):
                        ins = product(bank(b + a), (wgu_hi[:, par, a, k], wgu_lo[:, par, a, k]),
                                      (xT_hi[:, s, k], xT_lo[:, s, k]), k == 0, k == KC - 1)
                    ins.then_inc(ready, 1)

            def down(layer, n, g, par, start=False, stop=False):
                pe.wait_ge(g_ready, g + 1)
                pe.wait_ge(wd_lo_ready, g + 1)
                for t in range(TT):
                    if start:
                        wait_acc_free(pe, n, t)
                    low = g_lo[:, par, tok(t)] if layer == 0 else None
                    ins = product(acc[:, t], (g_hi[:, par, tok(t)], low), (wd_hi[:, par], wd_lo[:, par]), start, stop)
                    if stop:
                        ins.then_inc(acc_ready, 1)
                if not stop:
                    ins.then_inc(down_done, 1)

            def ffn(p):
                s, g0, layer = p % NSTREAM, NI * p, p // NSTREAM
                n = (2 if layer == 0 else 6) + s
                r0 = pass_bank(p)

                def gu(i, j=0, used=True):
                    gate_up(s, 2 * j + (g0 + i) if not isinstance(j, int) else g0 + i, (g0 + i) % 2, r0 + 2 * i, used)

                def dn(i, j=0, **kw):
                    down(layer, n, 2 * j + (g0 + i) if not isinstance(j, int) else g0 + i, (g0 + i) % 2, **kw)

                pe.wait_ge(xT_lo_ready, 4 * n + TT)
                gu(0, used=False)
                gu(1, used=False)
                gu(2)
                dn(0, start=True)
                with pe.Fori(0, (NI - 3) // 2) as j:
                    for h in range(2):
                        gu(3 + h, j)
                        dn(1 + h, j)
                dn(NI - 2)
                if n_in[p] is not None:
                    def free(t):
                        g = g0 + NI - 2 + t // 2
                        pe.wait_ge(silu_done if t % 2 == 0 else prod_ready, g + 1)
                    transposes(n_in[p], r0 + 2 * NI, free)
                dn(NI - 1, stop=True)

            def attention(s):
                r, n = pass_bank(2), 4 + s

                def v_tile(t):
                    for k in range(KC):
                        ins = product(bank(r + 2)[:, tok(t)], (xT_hi[:, s, k, tok(t)], xT_lo[:, s, k, tok(t)]),
                                      (wqkv_hi[:, k, tok(2)], wqkv_lo[:, k, tok(2)]), k == 0, k == KC - 1)
                    return ins

                def prob_transpose(t):
                    m = 4 * s + t
                    pe.wait_ge(prob_ready, m + 1)
                    for k in range(KC):
                        ins = nc.tensor.transpose(bank(r + 3 + t)[:, tok(k)], prob[:, m % 2, tok(k)], ident[:])
                    ins.then_inc(prob_transposed, 1)

                def mix(h):
                    q = slice(h * SEQ // 2, (h + 1) * SEQ // 2)
                    pe.wait_ge(pT_lo_ready, 4 * s + 2 * h + 2)
                    for k in range(KC):
                        ins = product(bank(r + 3)[:, q], (qkv_hi[:, 2, tok(k)], qkv_lo[:, 2, tok(k)]),
                                      (wide_hi[:, k, q], wide_lo[:, k, q]), k == 0, k == KC - 1)
                    ins.then_inc(mixed, 1)

                def project(t):
                    pe.wait_ge(oT_lo_ready, 2 * s + t // 2 + 1)
                    product(acc[:, t], (qkv_hi[:, 0, tok(t)], qkv_lo[:, 0, tok(t)]),
                            (wo_hi[:], wo_lo[:]), True, True).then_inc(acc_ready, 1)

                pe.wait_ge(xT_lo_ready, 4 * n + TT)
                pe.wait_ge(attw_lo_ready, 2)
                for q, a in enumerate((1, 0)):
                    for k in range(KC):
                        ins = product(bank(r + q), (wqkv_hi[:, k, tok(a)], wqkv_lo[:, k, tok(a)]),
                                      (xT_hi[:, s, k], xT_lo[:, s, k]), k == 0, k == KC - 1)
                    ins.then_inc(qk_prod, 1)
                v_tile(0)
                v_tile(1)
                pe.wait_ge(qk_lo_ready, 2 * s + 2)
                for t in range(TT):
                    wait_acc_free(pe, n, t)
                    product(acc[:, t], (qkv_hi[:, 0, tok(t)], qkv_lo[:, 0, tok(t)]),
                            (qkv_hi[:, 1], qkv_lo[:, 1]), True, True).then_inc(scored, 1)
                v_tile(2)
                v_tile(3).then_inc(v_prod, 1)
                prob_transpose(0)
                prob_transpose(1)
                prob_transpose(2)
                pe.wait_ge(v_lo_ready, s + 1)
                mix(0)
                prob_transpose(3)
                project(0)
                project(1)
                mix(1)

                def free(t):
                    if t == 3:
                        pe.wait_ge(oT_lo_ready, 2 * s + 2)
                transposes(n + 1, r, free)
                project(2)
                project(3)

            pe.wait_ge(const_loaded, 32)
            transposes(0, 0)
            pe.wait_ge(blk_summed, 1)
            nc.tensor.matmul(acc[:, 0, 0:KC * D // BLK], ones_blk[:], blk_rows[:], start=True, stop=True).then_inc(blk_spread, 1)
            pe.wait_ge(keep_ready, 1)
            linear(0, wide_hi, wide_lo, lambda: transposes(1, 0))
            linear(1, wide_hi, wide_lo)
            pe.wait_ge(xT_lo_ready, 8)
            transposes(2, 0)
            ffn(0)
            ffn(1)
            attention(0)
            attention(1)
            ffn(2)
            ffn(3)


def kernel(L0_attn_data, L0_attn_weight, L0_attn_mask, L0_ffn_w_gate, L0_ffn_b_gate, L0_ffn_w_up, L0_ffn_b_up,
           L0_ffn_w_down, L0_ffn_b_down, L1_attn_Wqkv, L1_attn_bqkv, L1_attn_Wo, L1_attn_bo, L1_ffn_w_gate,
           L1_ffn_w_up, L1_ffn_w_down):
    import numpy as np
    import concourse.bacc as bacc
    from concourse.bass_utils import run_bass_kernel_spmd

    def chunked(w):
        return np.asarray(w).reshape(KC, P, -1).transpose(1, 0, 2)

    def padded(w):
        w = np.asarray(w)
        return np.concatenate([w, np.zeros((NI * P - INTER,) + w.shape[1:], w.dtype)])

    def by_feature(w):
        return padded(w).reshape(NI, P, KC, P).transpose(0, 3, 2, 1)

    def columns(b):
        return padded(b).reshape(NI, P).T

    def rows(b):
        b = np.asarray(b)
        return np.broadcast_to(b, (P, b.size))

    bqkv = np.asarray(L1_attn_bqkv)
    gu = np.stack([np.stack([by_feature(a), by_feature(b)], axis=2)
                   for a, b in ((L0_ffn_w_gate, L0_ffn_w_up), (L1_ffn_w_gate, L1_ffn_w_up))])
    arrays = {
        "x_in": np.asarray(L0_attn_data).reshape(NSTREAM * TT, P, D),
        "w_mix": chunked(np.asarray(L0_attn_weight).T),
        "mask": chunked(np.asarray(L0_attn_mask).T),
        "ffn_gu": gu.reshape(2, NI, P, 2 * KC * P),
        "ffn_d": np.stack([padded(np.asarray(w).T).reshape(NI, P, D) for w in (L0_ffn_w_down, L1_ffn_w_down)]),
        "b_gate": columns(L0_ffn_b_gate),
        "b_up": columns(L0_ffn_b_up),
        "b_down": rows(L0_ffn_b_down),
        "w_qkv": chunked(L1_attn_Wqkv).reshape(P, KC * 3 * P),
        "b_qk": bqkv[:2 * P].reshape(2, P).T,
        "b_v": rows(bqkv[2 * P:]),
        "w_o": np.asarray(L1_attn_Wo),
        "b_o": rows(L1_attn_bo),
        "identity": np.eye(P, dtype=np.float32),
        "block_ones": np.kron(np.eye(P // BLK, dtype=np.float32), np.ones((BLK, BLK), np.float32)),
    }
    arrays = {f"{k}_dram": np.ascontiguousarray(a) for k, a in arrays.items()}
    nc = bacc.Bacc("TRN2", target_bir_lowering=False, num_devices=1)
    args = [nc.dram_tensor(k, a.shape, mybir.dt.from_np(a.dtype), kind="ExternalInput").ap()
            for k, a in arrays.items()]
    args.append(nc.dram_tensor("out_dram", (NSTREAM * TT, P, D), F32, kind="ExternalOutput").ap())
    build_two_layers(nc, *args)
    r = run_bass_kernel_spmd(nc, [arrays], core_ids=[0])
    return r.results[0]["out_dram"].reshape(NSTREAM, SEQ, D)
```

```python
from contextlib import ExitStack

import numpy as np

import concourse.bass as bass
from concourse import mybir

P = 128
D = 512
KC = D // P
SEQ = 512
TT = SEQ // P
NSTREAM = 2
INTER = 1376
NI = -(-INTER // P)
BLK = 32
EPS = 1e-5
QSCALE = 128.0
ATT_SCALE = 1.0 / float(P) ** 0.5
WARM_UP = 12
NPASS = 2 * NSTREAM

ALU = mybir.AluOpType
ACT = mybir.ActivationFunctionType
F32 = mybir.dt.float32
F32R = mybir.dt.float32r
BF16 = mybir.dt.bfloat16
I16 = mybir.dt.int16
I32 = mybir.dt.int32
AX = mybir.AxisListType.X


def build_two_layers(nc, x_in, w_mix, mask, ffn_gu, ffn_d, b_gate, b_up, b_down, w_qkv, b_qk, b_v,
                     w_o, b_o, identity, block_ones, out):
    with ExitStack() as ctx:
        def sb(name, shape, dt=F32):
            return ctx.enter_context(nc.sbuf_tensor(name, shape, dt))

        def sem(name):
            return ctx.enter_context(nc.semaphore(name))

        x = sb("x", [P, NSTREAM * TT, D])
        xT_hi = sb("xT_hi", [P, NSTREAM, KC, SEQ], F32R)
        xT_lo = sb("xT_lo", [P, NSTREAM, KC, SEQ], F32R)
        raw_gu = sb("raw_gu", [P, 2, 2 * KC * P])
        raw_d = sb("raw_d", [P, 2, D])
        wgu_hi = sb("wgu_hi", [P, 2, 2, KC, P], F32R)
        wgu_lo = sb("wgu_lo", [P, 2, 2, KC, P], F32R)
        wd_hi = sb("wd_hi", [P, 2, D], F32R)
        wd_lo = sb("wd_lo", [P, 2, D], F32R)
        sil = sb("sil", [P, 2, SEQ])
        prod = sb("prod", [P, 2, SEQ])
        g_hi = sb("g_hi", [P, 2, SEQ], F32R)
        g_lo = sb("g_lo", [P, 2, SEQ], F32R)
        z = sb("z", [P, TT, D])
        y = sb("y", [P, TT, D])
        mag = sb("mag", [P, SEQ])
        sgn = sb("sgn", [P, SEQ], BF16)
        rnd = sb("rnd", [P, 2, SEQ], I16)
        over = sb("over", [P, 2, SEQ], BF16)
        floor = sb("floor", [P, 2, SEQ], BF16)
        signed = sb("signed", [P, 2, SEQ], BF16)
        stage = sb("stage", [P, KC, D])
        maskb = sb("maskb", [P, KC, D], I32)
        wide_hi = sb("wide_hi", [P, KC, D], F32R)
        wide_lo = sb("wide_lo", [P, KC, D], F32R)
        wqkv_hi = sb("wqkv_hi", [P, KC, 3 * P], F32R)
        wqkv_lo = sb("wqkv_lo", [P, KC, 3 * P], F32R)
        wo_hi = sb("wo_hi", [P, D], F32R)
        wo_lo = sb("wo_lo", [P, D], F32R)
        qkv = sb("qkv", [P, 3, SEQ])
        qkv_hi = sb("qkv_hi", [P, 3, SEQ], F32R)
        qkv_lo = sb("qkv_lo", [P, 3, SEQ], F32R)
        prob = sb("prob", [P, TT, SEQ])
        out_mag = y
        out_sgn = prob[:].rearrange("p a b -> p (a b)").bitcast(BF16).rearrange("p (t b) -> p t b", t=TT)[:, :, 0:SEQ]
        early = qkv[:].rearrange("p a b -> p (a b)").bitcast(BF16).rearrange("p (a t b) -> p a t b", a=3, t=2)
        early_rnd, early_over, early_floor = early[:, 0].bitcast(I16), early[:, 1], early[:, 2]
        exp_scratch = sb("exp_scratch", [P, 1])
        ident = sb("ident", [P, P])
        ones_blk = sb("ones_blk", [P, P])
        blk_rows = sb("blk_rows", [P, KC, D // BLK])
        keep = sb("keep", [P, KC, D // BLK])
        bg = sb("bg", [P, NI])
        bu = sb("bu", [P, NI])
        bd = sb("bd", [P, D])
        bqk = sb("bqk", [P, 2])
        bv = sb("bv", [P, P])
        bo = sb("bo", [P, D])
        stats = sb("stats", [P, 2, TT, 6])
        mv = sb("mv", [P, 2, TT, 2])
        var_eps = sb("var_eps", [P, 2, TT])
        rstd = sb("rstd", [P, 2, TT])
        neg_mr = sb("neg_mr", [P, TT])
        neg_mr_in = sb("neg_mr_in", [P, TT])
        minus_half = sb("minus_half", [P, TT])
        row_max = sb("row_max", [P, TT])
        neg_max = sb("neg_max", [P, TT])
        row_sum = sb("row_sum", [P, TT])
        inv_sum = sb("inv_sum", [P, NSTREAM, TT])

        acc = ctx.enter_context(nc.psum_tensor("acc", [P, TT, D], F32))
        ring = ctx.enter_context(nc.psum_tensor("ring", [P, 4, 512], F32))

        x_loaded = [sem(f"x_loaded{t}") for t in range(NSTREAM * TT)]
        mask_loaded = [sem(f"mask_loaded{k}") for k in range(KC)]
        mix_loaded = [sem(f"mix_loaded{k}") for k in range(KC)]
        ident_loaded, ones_loaded, bias_loaded, attw_loaded = map(
            sem, ["ident_loaded", "ones_loaded", "bias_loaded", "attw_loaded"])
        gu_loaded = [sem(f"gu_loaded{i}") for i in range(2)]
        d_loaded = [sem(f"d_loaded{i}") for i in range(2)]
        stored = sem("stored")
        in_stats, in_aggr, in_var, in_rstd = map(sem, ["in_stats", "in_aggr", "in_var", "in_rstd"])
        y_ready, transposed, xT_hi_ready, xT_lo_ready = map(
            sem, ["y_ready", "transposed", "xT_hi_ready", "xT_lo_ready"])
        acc_ready, z_ready, out_stats, out_aggr, out_var, out_rstd, out_nmr, u_ready, x_updated = map(
            sem, ["acc_ready", "z_ready", "out_stats", "out_aggr", "out_var", "out_rstd", "out_nmr", "u_ready",
                  "x_updated"])
        in_nmr, x_shifted = sem("in_nmr"), sem("x_shifted")
        mag_ready, sgn_ready, out_mag_ready, out_sgn_ready, early_step, centred, x_updated_last = map(
            sem, ["mag_ready", "sgn_ready", "out_mag_ready", "out_sgn_ready", "early_step", "centred",
                  "x_updated_last"])
        zeros_set, half_set = sem("zeros_set"), sem("half_set")
        blk_summed, blk_spread, keep_ready, masked, mix_hi_ready = map(
            sem, ["blk_summed", "blk_spread", "keep_ready", "masked", "mix_hi_ready"])
        mix_lo_ready = [sem(f"mix_lo_ready{k}") for k in range(KC)]
        wgu_hi_ready, wgu_lo_ready, wd_hi_ready, wd_lo_ready = map(
            sem, ["wgu_hi_ready", "wgu_lo_ready", "wd_hi_ready", "wd_lo_ready"])
        gate_ready, up_ready, down_done, silu_done, prod_ready, g_hi_ready, g_ready, trunc_step = map(
            sem, ["gate_ready", "up_ready", "down_done", "silu_done", "prod_ready", "g_hi_ready",
                  "g_ready", "trunc_step"])
        attw_hi_ready, attw_lo_ready = sem("attw_hi_ready"), sem("attw_lo_ready")
        qk_prod, qk_full, qk_hi_ready, qk_lo_ready = map(sem, ["qk_prod", "qk_full", "qk_hi_ready", "qk_lo_ready"])
        v_prod, v_full, v_hi_ready, v_lo_ready = map(sem, ["v_prod", "v_full", "v_hi_ready", "v_lo_ready"])
        scored, maxed, max_scaled, exp_done, sum_inverted = map(
            sem, ["scored", "maxed", "max_scaled", "exp_done", "sum_inverted"])
        prob_transposed, pT_hi_ready, pT_lo_ready = map(
            sem, ["prob_transposed", "pT_hi_ready", "pT_lo_ready"])
        mixed, oT_hi_ready, oT_lo_ready = map(sem, ["mixed", "oT_hi_ready", "oT_lo_ready"])

        def f32(ap):
            return ap.bitcast(F32)

        def pass_bank(p):
            return (2 * NI * p) % 4

        def bank(r):
            return ring[:, r % 4, :]

        def tok(t):
            return slice(t * P, (t + 1) * P)

        def wait_acc_free(eng, n, t):
            if 1 <= n <= 6:
                eng.wait_ge(z_ready, 4 * (n - 1) + t + 1)
            elif n == 7:
                eng.wait_ge(out_sgn_ready, t // 2 + 1)

        def wait_down(eng, p, i, off=0):
            if i == 1 and p > 0:
                eng.wait_ge(acc_ready, 4 * (p + 1 if p <= NSTREAM else p + 3) + TT)
            elif i >= 2 or p > 0:
                eng.wait_ge(down_done, off + ((NI - 1) * p + max(i - 1, 0)))

        def in_count(n):
            return n + 1 + (n >= 0) + (n >= 2) + (n >= 5) + (n >= 6)

        def out_count(n):
            return n + 1 + (n >= 0) + (n >= 7)

        def u_count(n, t):
            return 4 * (n - 1) + t + 1

        halves = ((NI - 2, 0), (NI - 1, 0), (NI - 2, 1), (NI - 1, 1))

        def half(h):
            return slice(h * SEQ // 2, (h + 1) * SEQ // 2)

        n_out = [1, 2, 5, 6]
        n_in = [3, 4, 7, None]
        block = ctx.enter_context(nc.Block())

        @block.sync
        def _(sp):
            for t in range(TT):
                sp.dma_start(x[:, t], x_in[t]).then_inc(x_loaded[t], 16)
                if t == 1:
                    sp.dma_start(ident[:], identity).then_inc(ident_loaded, 16)
            sp.dma_start(ones_blk[:], block_ones).then_inc(ones_loaded, 16)
            sp.dma_start(maskb[:, 0], mask[:, 0]).then_inc(mask_loaded[0], 16)
            sp.dma_start(stage[:, 0], w_mix[:, 0]).then_inc(mix_loaded[0], 16)
            for k in range(1, KC):
                sp.dma_start(maskb[:, k], mask[:, k]).then_inc(mask_loaded[k], 16)
            for k in range(1, KC):
                sp.dma_start(stage[:, k], w_mix[:, k]).then_inc(mix_loaded[k], 16)
            for t in range(TT, 2 * TT):
                sp.dma_start(x[:, t], x_in[t]).then_inc(x_loaded[t], 16)
            for i in range(2):
                sp.dma_start(raw_gu[:, i], ffn_gu[0, i]).then_inc(gu_loaded[i], 16)
            for i in range(2):
                sp.dma_start(raw_d[:, i], ffn_d[0, i]).then_inc(d_loaded[i], 16)
            for dst, src in ((bg, b_gate), (bu, b_up), (bd, b_down), (bqk, b_qk), (bv, b_v), (bo, b_o)):
                sp.dma_start(dst[:], src).then_inc(bias_loaded, 16)
            sp.wait_ge(masked, KC)
            sp.dma_start(stage[:, 0:3].rearrange("p a b -> p (a b)"), w_qkv).then_inc(attw_loaded, 16)
            sp.dma_start(stage[:, 3], w_o).then_inc(attw_loaded, 16)

            def load_gu(layer, i, g, par):
                sp.wait_ge(wgu_lo_ready, g - 1)
                sp.dma_start(raw_gu[:, par], ffn_gu[layer, i]).then_inc(gu_loaded[par], 16)

            def load_d(layer, i, g, par):
                sp.wait_ge(wd_lo_ready, g - 1)
                sp.dma_start(raw_d[:, par], ffn_d[layer, i]).then_inc(d_loaded[par], 16)

            for p in range(NPASS):
                g0, layer = NI * p, p // NSTREAM

                def load(i):
                    if p > 0 or i >= 2:
                        load_d(layer, i, g0 + i, (g0 + i) % 2)
                    if i + 2 < NI:
                        load_gu(layer, i + 2, g0 + i + 2, (g0 + i) % 2)
                    elif p + 1 < NPASS:
                        load_gu((p + 1) // NSTREAM, i + 2 - NI, g0 + i + 2, (g0 + i) % 2)

                load(0)
                load(1)
                with sp.Fori(0, (NI - 5) // 2) as j:
                    for i in (2, 3):
                        load_d(layer, 2 * j + i, 2 * j + (g0 + i), (g0 + i) % 2)
                        load_gu(layer, 2 * j + (i + 2), 2 * j + (g0 + i + 2), (g0 + i) % 2)
                for i in range(NI - 3, NI):
                    load(i)
            for t in range(NSTREAM * TT):
                if TT <= t < TT + 2:
                    sp.wait_ge(x_updated_last, t - TT + 1)
                else:
                    sp.wait_ge(x_updated, 3 * NSTREAM * TT + t + 1 - (2 if t >= TT else 0))
                sp.dma_start(out[t], x[:, t]).then_inc(stored, 16)
            sp.wait_ge(stored, 16 * NSTREAM * TT)

        @block.gpsimd
        def _(pool):
            G = nc.gpsimd
            G.memset(sgn[:], 0.0).then_inc(zeros_set, 1)
            G.memset(minus_half[:], -0.5).then_inc(half_set, 1)
            pool.wait_ge(half_set, 1)

            def before(n):
                pool.wait_ge(in_var, in_count(n))
                G.tensor_tensor(rstd[:, 0], var_eps[:, 0], minus_half[:], ALU.pow).then_inc(in_rstd, 1)

            def after(n):
                pool.wait_ge(out_var, out_count(n))
                G.tensor_tensor(rstd[:, 1], var_eps[:, 1], minus_half[:], ALU.pow).then_inc(out_rstd, 1)

            def by_pairs(a, h, var, done, count):
                q = slice(2 * h, 2 * h + 2)
                pool.wait_ge(var, count)
                return G.tensor_tensor(rstd[:, a, q], var_eps[:, a, q], minus_half[:, q], ALU.pow).then_inc(done, 1)

            def split_gu_lo(g, par):
                pool.wait_ge(wgu_hi_ready, g + 1)
                G.tensor_tensor(wgu_lo[:, par].rearrange("p a k m -> p (a k m)"), raw_gu[:, par],
                                f32(wgu_hi[:, par].rearrange("p a k m -> p (a k m)")),
                                ALU.subtract).then_inc(wgu_lo_ready, 1)

            def split_d_lo(g, par):
                pool.wait_ge(wd_hi_ready, g + 1)
                G.tensor_tensor(wd_lo[:, par], raw_d[:, par], f32(wd_hi[:, par]), ALU.subtract).then_inc(wd_lo_ready, 1)

            def tile(g, par, ahead=True):
                if ahead:
                    split_gu_lo(g + 2, par)
                split_d_lo(g, par)

            def ffn(p):
                g0, last = NI * p, p == NPASS - 1
                if not last:
                    after(n_out[p])
                for i in range(3):
                    tile(g0 + i, (g0 + i) % 2)
                if last:
                    after(n_out[p])
                else:
                    before(n_in[p])
                if p == 0:
                    pool.wait_ge(attw_hi_ready, 1)
                    G.tensor_tensor(wqkv_lo[:].rearrange("p k m -> p (k m)"), stage[:, 0:3].rearrange("p a b -> p (a b)"),
                                    f32(wqkv_hi[:].rearrange("p k m -> p (k m)")), ALU.subtract).then_inc(attw_lo_ready, 1)
                    pool.wait_ge(attw_hi_ready, 2)
                    G.tensor_tensor(wo_lo[:], stage[:, 3], f32(wo_hi[:]), ALU.subtract).then_inc(attw_lo_ready, 1)
                with pool.Fori(0, (NI - 3) // 2 - last) as j:
                    for h in (3, 4):
                        tile(2 * j + (g0 + h), (g0 + h) % 2)
                if last:
                    for i in (NI - 2, NI - 1):
                        tile(g0 + i, (g0 + i) % 2, ahead=False)

            def attention(s):
                n = 3 + s

                def residual(t):
                    pool.wait_ge(u_ready, u_count(n, t))
                    x_t = x[:, 4 * (n % 2) + t]
                    G.tensor_tensor(x_t, x_t, z[:, t], ALU.add).then_inc(x_updated, 1)

                def v_low(h):
                    c = half(h)
                    pool.wait_ge(v_hi_ready, 2 * s + h + 1)
                    G.tensor_tensor(qkv_lo[:, 2, c], qkv[:, 2, c], f32(qkv_hi[:, 2, c]),
                                    ALU.subtract).then_inc(v_lo_ready, 1)

                pool.wait_ge(qk_hi_ready, 2 * s + 1)
                G.tensor_tensor(qkv_lo[:, 1], qkv[:, 1], f32(qkv_hi[:, 1]), ALU.subtract).then_inc(qk_lo_ready, 1)
                after(n)
                residual(0)
                residual(1)
                v_low(0)
                residual(2)
                residual(3)
                v_low(1)
                by_pairs(0, 0, in_var, in_rstd, in_count(n + 1) + 1)
                by_pairs(0, 1, in_var, in_rstd, in_count(n + 1) + 2)

            for h in range(2):
                by_pairs(0, h, in_var, in_rstd, h + 1)
            for k in range(KC):
                pool.wait_ge(keep_ready, k + 1)
                pool.wait_ge(mix_loaded[k], 16)
                G.tensor_tensor(f32(maskb[:, k]).rearrange("p (b c) -> p b c", c=BLK),
                                stage[:, k].rearrange("p (b c) -> p b c", c=BLK),
                                keep[:, k].unsqueeze(2).broadcast_to([P, D // BLK, BLK]), ALU.mult).then_inc(masked, 1)
            for k in range(KC // 2, KC):
                pool.wait_ge(mix_hi_ready, k + 1)
                G.tensor_tensor(wide_lo[:, k], f32(maskb[:, k]), f32(wide_hi[:, k]),
                                ALU.subtract).then_inc(mix_lo_ready[k], 1)
            before(1)
            for g in range(2):
                split_gu_lo(g, g)
            for h in range(2):
                by_pairs(1, h, out_var, out_rstd, h + 1)
            for h in range(2):
                by_pairs(0, h, in_var, in_rstd, in_count(1) + h + 1)
            ffn(0)
            ffn(1)
            attention(0)
            attention(1)
            ffn(2)
            ffn(3)
            by_pairs(1, 0, out_var, out_rstd, out_count(6) + 1)

            def residual_last(t):
                pool.wait_ge(u_ready, u_count(7, t))
                G.tensor_tensor(x[:, TT + t], x[:, TT + t], z[:, t], ALU.add).then_inc(x_updated_last, 1)

            residual_last(0)
            residual_last(1)
            by_pairs(1, 1, out_var, out_rstd, out_count(6) + 2)

        @block.scalar
        def _(act):
            def split_gu_hi(g, par):
                act.wait_ge(gu_loaded[par], (g // 2 + 1) * 16 if isinstance(g, int) else g * 8 + (16 - 8 * par))
                src = raw_gu[:, par].rearrange("p (a b) -> p a b", a=2)
                nc.scalar.copy(wgu_hi[:, par].rearrange("p a k m -> p a (k m)"), src).then_inc(wgu_hi_ready, 1)

            def split_d_hi(g, par):
                act.wait_ge(d_loaded[par], (g // 2 + 1) * 16 if isinstance(g, int) else g * 8 + (16 - 8 * par))
                nc.scalar.copy(wd_hi[:, par], raw_d[:, par]).then_inc(wd_hi_ready, 1)

            def xT_hi_tiles(n, r, tiles=range(TT)):
                s = n % 2
                for t in tiles:
                    act.wait_ge(transposed, 4 * n + t + 1)
                    nc.scalar.copy(xT_hi[:, s, :, tok(t)],
                                   bank(r + t).rearrange("p (k m) -> p k m", k=KC)).then_inc(xT_hi_ready, 1)

            def scale_before(n, tiles):
                for t in tiles:
                    if n > 0:
                        act.wait_ge(transposed, 4 * (n - 1) + t + 1)
                    nc.scalar.activation(y[:, t], x[:, 4 * (n % 2) + t], ACT.Identity, bias=neg_mr_in[:, t:t + 1],
                                         scale=rstd[:, 0, t:t + 1]).then_inc(y_ready, 1)

            def copy_result(n):
                for t in range(TT):
                    act.wait_ge(acc_ready, 4 * n + t + 1)
                    if n >= 1:
                        act.wait_ge(x_updated, 4 * (n - 1) + t + 1)
                    nc.scalar.copy(z[:, t], acc[:, t]).then_inc(z_ready, 1)

            def normalise(n, tiles=range(TT)):
                for t in tiles:
                    act.wait_ge(out_nmr, n + 1)
                    nc.scalar.activation(z[:, t], z[:, t], ACT.Identity, bias=neg_mr[:, t:t + 1],
                                         scale=rstd[:, 1, t:t + 1]).then_inc(u_ready, 1)

            def result_magnitude(n, h):
                q = slice(2 * h, 2 * h + 2)
                act.wait_ge(acc_ready, 4 * n + 2 * h + 2)
                if n == 6:
                    act.wait_ge(transposed, 4 * 8)
                else:
                    act.wait_ge(z_ready, 4 * 6 + 4)
                nc.scalar.activation(out_mag[:, q], acc[:, q], ACT.Abs, scale=QSCALE).then_inc(out_mag_ready, 1)

            def result_sign(h):
                q = slice(2 * h, 2 * h + 2)
                nc.scalar.activation(out_sgn[:, q], acc[:, q], ACT.Sign).then_inc(out_sgn_ready, 1)

            def tile(p, i, par, b, first=False, ahead=True, j=None, q=None):
                layer, down_wait = p // NSTREAM, (p, i, 0 if j is None else 2 * j)
                g = NI * p + (i if q is None else NI - 2 + q)
                c = slice(0, SEQ) if q is None else half(halves[q][1])
                if j is not None:
                    i, g = 2 * j + i, 2 * j + g
                act.wait_ge(gate_ready, g + 1)
                if not first:
                    act.wait_ge(prod_ready, g - 1)
                if layer == 0:
                    nc.scalar.activation(sil[:, par], bank(b), ACT.Silu, bias=bg[:, bass.ds(i, 1)]).then_inc(silu_done, 1)
                else:
                    nc.scalar.activation(sil[:, par, c], bank(b)[:, c], ACT.Silu, scale=1.0 / QSCALE).then_inc(silu_done, 1)
                if ahead:
                    act.wait_ge(up_ready, g + 1)
                    split_gu_hi(g + 2, par)
                if layer == 0:
                    wait_down(act, *down_wait)
                    act.wait_ge(prod_ready, g + 1)
                    nc.scalar.copy(g_hi[:, par], prod[:, par]).then_inc(g_hi_ready, 1)
                else:
                    act.wait_ge(prod_ready, g + 1)
                    act.wait_ge(g_ready, g)
                    nc.scalar.activation(mag[:, c], prod[:, par, c], ACT.Abs).then_inc(mag_ready, 1)
                    nc.scalar.activation(sgn[:, c], prod[:, par, c], ACT.Sign).then_inc(sgn_ready, 1)
                    wait_down(act, *down_wait)
                if q is None or q < 2:
                    split_d_hi(g, par)

            def ffn(p):
                g0, layer, last = NI * p, p // NSTREAM, p == NPASS - 1
                r0 = pass_bank(p)
                if last:
                    for h in range(2):
                        result_magnitude(6, h)
                    for h in range(2):
                        result_sign(h)
                tile(p, 0, g0 % 2, r0, first=p == 0)
                if not last:
                    normalise(n_out[p])
                for i in (1, 2):
                    tile(p, i, (g0 + i) % 2, r0 + 2 * i, first=p == 0 and i < 2)
                if last:
                    normalise(6, (0, 1))
                    for i in (3, 4):
                        tile(p, i, (g0 + i) % 2, r0 + 2 * i)
                        normalise(6, (i - 1,))
                if p == 0:
                    act.wait_ge(attw_loaded, 32)
                    nc.scalar.copy(wqkv_hi[:].rearrange("p k m -> p (k m)"),
                                   stage[:, 0:3].rearrange("p a b -> p (a b)")).then_inc(attw_hi_ready, 1)
                    nc.scalar.copy(wo_hi[:], stage[:, 3]).then_inc(attw_hi_ready, 1)
                with act.Fori(int(last), (NI - 3) // 2 - last) as j:
                    for h in (3, 4):
                        tile(p, h, (g0 + h) % 2, r0 + 2 * h, j=j)
                if last:
                    for q, (i, _) in enumerate(halves):
                        if q == 3:
                            result_magnitude(7, 0)
                        tile(p, i, (g0 + i) % 2, r0 + 2 * i, ahead=False, q=q)
                if n_in[p] is not None:
                    xT_hi_tiles(n_in[p], r0 + 2 * NI)

            def attention(s):
                r = pass_bank(2)
                for q, a in enumerate((1, 0)):
                    act.wait_ge(qk_prod, 2 * s + q + 1)
                    if s:
                        act.wait_ge(qk_lo_ready, 2)
                    nc.scalar.activation(qkv[:, a], bank(r + q), ACT.Identity, bias=bqk[:, a:a + 1]).then_inc(qk_full, 1)
                    act.wait_ge(qk_full, 2 * s + q + 1)
                    nc.scalar.copy(qkv_hi[:, a], qkv[:, a]).then_inc(qk_hi_ready, 1)
                    if q == 0:
                        act.wait_ge(half_set, 1)
                        nc.scalar.activation(exp_scratch[:], minus_half[:, 0:1], ACT.Exp)

                def exp(t):
                    m = 4 * s + t
                    act.wait_ge(max_scaled, m + 1)
                    if s:
                        act.wait_ge(prob_transposed, m - TT + 1)
                    nc.scalar.activation(prob[:, t], acc[:, t], ACT.Exp, bias=neg_max[:, t:t + 1],
                                         scale=ATT_SCALE, accum_out=row_sum[:, t:t + 1]).then_inc(exp_done, 1)

                def pT_hi(t):
                    act.wait_ge(prob_transposed, 4 * s + t + 1)
                    nc.scalar.copy(wide_hi[:, :, tok(t)],
                                   bank(r + 3 + t).rearrange("p (k m) -> p k m", k=KC)).then_inc(pT_hi_ready, 1)

                def oT_hi(h):
                    act.wait_ge(mixed, 2 * s + h + 1)
                    c = half(h)
                    nc.scalar.copy(qkv_hi[:, 0, c], acc[:, 3 - h, c]).then_inc(oT_hi_ready, 1)

                def v_hi(h):
                    act.wait_ge(v_full, 2 * s + h + 1)
                    c = half(h)
                    nc.scalar.copy(qkv_hi[:, 2, c], qkv[:, 2, c]).then_inc(v_hi_ready, 1)

                normalise(3 + s, (0, 1))
                v_hi(0)
                normalise(3 + s, (2, 3))
                for t in range(TT):
                    exp(t)
                pT_hi(0)
                v_hi(1)
                for t in range(1, TT):
                    pT_hi(t)
                oT_hi(0)
                act.wait_ge(in_nmr, 4 + s)
                scale_before(5 + s, (0, 1))
                oT_hi(1)
                xT_hi_tiles(5 + s, r)

            for h in range(2):
                act.wait_ge(in_nmr, h + 1)
                scale_before(0, (2 * h, 2 * h + 1))
                if h == 0:
                    xT_hi_tiles(0, 0, (0,))
            for k in range(KC):
                act.wait_ge(masked, k + 1)
                nc.scalar.copy(wide_hi[:, k], f32(maskb[:, k])).then_inc(mix_hi_ready, 1)
                if k < 2:
                    xT_hi_tiles(0, 0, ((1, 2), (3,))[k])
            for g in range(2):
                split_gu_hi(g, g)
            xT_hi_tiles(1, 0)
            copy_result(0)
            act.wait_ge(in_nmr, 3)
            scale_before(2, (0, 1))
            xT_hi_tiles(2, 0)
            copy_result(1)
            act.wait_ge(out_nmr, 1)
            for t in range(TT):
                nc.scalar.activation(x[:, t], x[:, t], ACT.Identity, bias=neg_mr[:, t:t + 1]).then_inc(x_shifted, 1)
            act.wait_ge(bias_loaded, 16 * 6)
            ffn(0)
            ffn(1)
            attention(0)
            attention(1)
            ffn(2)
            ffn(3)
            result_sign(0)
            result_magnitude(7, 1)
            result_sign(1)
            normalise(7, (0, 1))

        @block.vector
        def _(dve):
            V = nc.vector

            def in_stats_tile(n, t):
                s = n % 2
                if n < 2:
                    dve.wait_ge(x_loaded[4 * s + t], 16)
                else:
                    dve.wait_ge(x_updated, 4 * (n - 2) + t + 1)
                V.bn_stats(stats[:, 0, t], x[:, 4 * s + t]).then_inc(in_stats, 1)

            def stats_before(n):
                for t in range(TT):
                    in_stats_tile(n, t)
                variance(0, n, range(TT))

            def variance(a, n, tiles):
                counted, aggr, var = ((in_stats, in_aggr, in_var), (out_stats, out_aggr, out_var))[a]
                for t in tiles:
                    dve.wait_ge(counted, 4 * n + t + 1)
                    V.bn_aggr(mv[:, a, t], stats[:, a, t]).then_inc(aggr, 1)
                dve.wait_ge(aggr, 4 * n + tiles[-1] + 1)
                q = slice(tiles[0], tiles[-1] + 1)
                V.tensor_scalar(var_eps[:, a, q], mv[:, a, q, 1], EPS, None, ALU.add).then_inc(var, 1)

            def shift_before(n, tiles, count):
                q = slice(tiles[0], tiles[-1] + 1)
                dve.wait_ge(in_rstd, count)
                V.scalar_tensor_tensor(out=neg_mr_in[:, q], in0=mv[:, 0, q, 0], scalar=-1.0, in1=rstd[:, 0, q],
                                       op0=ALU.mult, op1=ALU.mult).then_inc(in_nmr, 1)

            def scale_before(n, tiles=range(TT)):
                dve.wait_ge(in_rstd, in_count(n))
                for t in tiles:
                    if n >= 1:
                        dve.wait_ge(transposed, 4 * (n - 1) + t + 1)
                    V.tensor_scalar(y[:, t], x[:, 4 * (n % 2) + t], mv[:, 0, t, 0:1], rstd[:, 0, t:t + 1],
                                    ALU.subtract, ALU.mult).then_inc(y_ready, 1)

            def xT_low(n, r, tiles=range(TT)):
                s = n % 2
                for t in tiles:
                    dve.wait_ge(xT_hi_ready, 4 * n + t + 1)
                    V.tensor_tensor(xT_lo[:, s, :, tok(t)], bank(r + t).rearrange("p (k m) -> p k m", k=KC),
                                    f32(xT_hi[:, s, :, tok(t)]), ALU.subtract).then_inc(xT_lo_ready, 1)

            def truncate(mag_ap, sgn_ap, dst, u, count, done, wait_sgn, dst_free):
                V.tensor_scalar(rnd[u], mag_ap, 128.0, None, ALU.min).then_inc(trunc_step, 1)
                dve.wait_ge(trunc_step, count + 1)
                V.tensor_tensor(over[u], mag_ap, rnd[u], ALU.is_lt).then_inc(trunc_step, 1)
                dve.wait_ge(trunc_step, count + 2)
                V.tensor_tensor(floor[u], rnd[u], over[u], ALU.subtract).then_inc(trunc_step, 1)
                dve.wait_ge(trunc_step, count + 3)
                wait_sgn()
                V.tensor_tensor(signed[u], floor[u], sgn_ap, ALU.mult).then_inc(trunc_step, 1)
                dve.wait_ge(trunc_step, count + 4)
                dst_free()
                V.tensor_scalar(dst, signed[u], 127.0, None, ALU.min).then_inc(*done)

            def truncate_result(n, h, between=lambda: None):
                q = slice(2 * h, 2 * h + 2)
                m = 2 * (n - 6) + h + 1

                def wait_sgn():
                    between()
                    dve.wait_ge(out_sgn_ready, m)

                def z_free():
                    if n == 7:
                        dve.wait_ge(x_updated, 4 * 6 + 2 * h + 2)

                dve.wait_ge(out_mag_ready, m)
                truncate(out_mag[:, q], out_sgn[:, q], z[:, q], np.s_[:, 0:2], trunc_count(n, h), (z_ready, 2),
                         wait_sgn, z_free)

            def result_stats(n, t):
                dve.wait_ge(z_ready, 4 * n + t + 1)
                V.bn_stats(stats[:, 1, t], z[:, t]).then_inc(out_stats, 1)

            def evacuate(n):
                if n >= 2:
                    for t in range(TT):
                        dve.wait_ge(acc_ready, 4 * n + t + 1)
                        if n in (4, 5):
                            dve.wait_ge(sum_inverted, n - 3)
                            V.scalar_tensor_tensor(out=z[:, t], in0=acc[:, t], scalar=inv_sum[:, n - 4, t:t + 1],
                                                   in1=bo[:], op0=ALU.mult, op1=ALU.add).then_inc(z_ready, 1)
                        else:
                            V.tensor_tensor(z[:, t], acc[:, t], bd[:], ALU.add).then_inc(z_ready, 1)
                for t in range(TT):
                    result_stats(n, t)
                variance(1, n, range(TT))

            def shift_after(n):
                dve.wait_ge(out_rstd, out_count(n))
                V.scalar_tensor_tensor(out=neg_mr[:], in0=mv[:, 1, :, 0], scalar=-1.0, in1=rstd[:, 1],
                                       op0=ALU.mult, op1=ALU.mult).then_inc(out_nmr, 1)

            def residual(n, tiles=range(TT)):
                s = n % 2
                for t in tiles:
                    dve.wait_ge(u_ready, u_count(n, t))
                    if n == 2:
                        dve.wait_ge(x_shifted, t + 1)
                    V.tensor_tensor(x[:, 4 * s + t], x[:, 4 * s + t], z[:, t], ALU.add).then_inc(x_updated, 1)

            def trunc_count(n, h):
                return 4 * (2 * NI + 4) if n == 7 else 4 * (NI + 2 * h)

            def pass_trunc_count(p, i):
                return 4 * i if p == 2 else 4 * (NI + i + (2 if i >= 1 else 1))

            def tile(p, i, par, b, first=False, truncs=0, j=None, q=None):
                layer, down_wait = p // NSTREAM, (p, i, 0 if j is None else 2 * j)
                g = NI * p + (i if q is None else NI - 2 + q)
                c = slice(0, SEQ) if q is None else half(halves[q][1])
                if j is not None:
                    i, g = 2 * j + i, 2 * j + g
                dve.wait_ge(silu_done, g + 1)
                dve.wait_ge(up_ready, g + 1)
                if layer == 0:
                    if not first:
                        dve.wait_ge(g_ready, g - 1)
                    V.scalar_tensor_tensor(out=prod[:, par], in0=bank(b + 1), scalar=bu[:, bass.ds(i, 1)],
                                           in1=sil[:, par], op0=ALU.add, op1=ALU.mult).then_inc(prod_ready, 1)
                else:
                    dve.wait_ge(g_ready, g - 1)
                    V.tensor_tensor(prod[:, par, c], bank(b + 1)[:, c], sil[:, par, c], ALU.mult).then_inc(prod_ready, 1)
                if layer == 0:
                    dve.wait_ge(g_hi_ready, g + 1)
                    V.tensor_tensor(g_lo[:, par], prod[:, par], f32(g_hi[:, par]), ALU.subtract).then_inc(g_ready, 1)
                else:
                    dve.wait_ge(mag_ready, g - (NSTREAM * NI - 1))
                    truncate(mag[:, c], sgn[:, c], g_hi[:, par, c], np.s_[:, 0, c], truncs, (g_ready, 1),
                             lambda: dve.wait_ge(sgn_ready, g - (NSTREAM * NI - 1)),
                             lambda: wait_down(dve, *down_wait))

            def early_result(part):
                if part == 0:
                    dve.wait_ge(out_mag_ready, 3)
                    V.tensor_scalar(early_rnd, out_mag[:, 0:2], 128.0, None, ALU.min).then_inc(early_step, 1)
                    dve.wait_ge(early_step, 1)
                    V.tensor_tensor(early_over, out_mag[:, 0:2], early_rnd, ALU.is_lt).then_inc(early_step, 1)
                else:
                    dve.wait_ge(early_step, 2)
                    V.tensor_tensor(early_floor, early_rnd, early_over, ALU.subtract).then_inc(early_step, 1)
                    dve.wait_ge(early_step, 3)
                    dve.wait_ge(out_sgn_ready, 3)
                    V.tensor_tensor(early_over, early_floor, out_sgn[:, 0:2], ALU.mult).then_inc(early_step, 1)
                    dve.wait_ge(early_step, 4)
                    dve.wait_ge(x_updated, 4 * 6 + 2)
                    V.tensor_scalar(z[:, 0:2], early_over, 127.0, None, ALU.min).then_inc(z_ready, 2)

            def ffn(p):
                g0, last = NI * p, p == NPASS - 1
                r0 = pass_bank(p)

                def one(i):
                    tile(p, i, (g0 + i) % 2, r0 + 2 * i, first=p == 0 and i < 2,
                         truncs=pass_trunc_count(p, i) if p >= 2 else 0)

                if last:
                    truncate_result(6, 0)
                    one(0)
                    truncate_result(6, 1)
                    one(1)
                    for t in range(TT):
                        result_stats(6, t)
                    variance(1, 6, range(TT))
                    one(2)
                    shift_after(6)
                else:
                    evacuate(n_out[p])
                    one(0)
                    shift_after(n_out[p])
                    one(1)
                    residual(n_out[p])
                    stats_before(n_in[p])
                    one(2)
                    scale_before(n_in[p])
                if last:
                    one(3)
                    residual(6, (0, 1))
                    one(4)
                    residual(6, (2, 3))
                with dve.Fori(int(last), (NI - 3) // 2 - last) as j:
                    for h in (3, 4):
                        tile(p, h, (g0 + h) % 2, r0 + 2 * h,
                             truncs=8 * j + pass_trunc_count(p, h) if p >= 2 else 0, j=j)
                if last:
                    for q, (i, _) in enumerate(halves):
                        if q == 3:
                            early_result(0)
                        tile(p, i, (g0 + i) % 2, r0 + 2 * i, truncs=pass_trunc_count(p, NI - 2 + q), q=q)
                else:
                    xT_low(n_in[p], r0 + 2 * NI)

            def attention(s):
                r, c = pass_bank(2), 3 + s

                def softmax_max(t):
                    m = 4 * s + t
                    q = slice(t, t + 1)
                    dve.wait_ge(scored, m + 1)
                    V.reduce_max(row_max[:, q], acc[:, t], AX).then_inc(maxed, 1)
                    dve.wait_ge(maxed, m + 1)
                    V.tensor_scalar(neg_max[:, q], row_max[:, q], -ATT_SCALE, None, ALU.mult).then_inc(max_scaled, 1)

                def v_bias(h):
                    c, t = half(h), TT // 2
                    dve.wait_ge(v_prod, 2 * s + h + 1)
                    V.tensor_tensor(qkv[:, 2, c].rearrange("p (t d) -> p t d", t=t),
                                    bank(r + 2)[:, c].rearrange("p (t d) -> p t d", t=t),
                                    bv[:].unsqueeze(1).broadcast_to([P, t, P]), ALU.add).then_inc(v_full, 1)

                def pT_low(t):
                    dve.wait_ge(pT_hi_ready, 4 * s + t + 1)
                    V.tensor_tensor(wide_lo[:, :, tok(t)], bank(r + 3 + t).rearrange("p (k m) -> p k m", k=KC),
                                    f32(wide_hi[:, :, tok(t)]), ALU.subtract).then_inc(pT_lo_ready, 1)

                def oT_low(h):
                    dve.wait_ge(oT_hi_ready, 2 * s + h + 1)
                    q = half(h)
                    V.tensor_tensor(qkv_lo[:, 0, q], acc[:, 3 - h, q], f32(qkv_hi[:, 0, q]),
                                    ALU.subtract).then_inc(oT_lo_ready, 1)

                evacuate(c)
                dve.wait_ge(qk_hi_ready, 2 * s + 2)
                V.tensor_tensor(qkv_lo[:, 0], qkv[:, 0], f32(qkv_hi[:, 0]), ALU.subtract).then_inc(qk_lo_ready, 1)
                shift_after(c)
                v_bias(0)
                for t in range(TT):
                    softmax_max(t)
                in_stats_tile(c + 2, 0)
                in_stats_tile(c + 2, 1)
                v_bias(1)
                variance(0, c + 2, (0, 1))
                pT_low(0)
                pT_low(1)
                in_stats_tile(c + 2, 2)
                shift_before(c + 2, (0, 1), in_count(c + 1) + 1)
                dve.wait_ge(exp_done, 4 * s + TT)
                V.reciprocal(inv_sum[:, s], row_sum[:]).then_inc(sum_inverted, 1)
                pT_low(2)
                pT_low(3)
                oT_low(0)
                in_stats_tile(c + 2, 3)
                variance(0, c + 2, (2, 3))
                oT_low(1)
                dve.wait_ge(y_ready, 4 * (c + 2) + 2)
                scale_before(c + 2, (2, 3))
                xT_low(c + 2, r)

            def sum_blocks(k):
                dve.wait_ge(mask_loaded[k], 16)
                V.reduce_sum(blk_rows[:, k], maskb[:, k].rearrange("p (b c) -> p b c", c=BLK), AX).then_inc(blk_summed, 1)

            def keep_blocks(k):
                dve.wait_ge(blk_spread, k + 1)
                V.tensor_scalar(keep[:, k], acc[:, k, 0:D // BLK], 0.0, None, ALU.is_gt).then_inc(keep_ready, 1)

            def mix_low(k):
                dve.wait_ge(mix_hi_ready, k + 1)
                V.tensor_tensor(wide_lo[:, k], f32(maskb[:, k]), f32(wide_hi[:, k]),
                                ALU.subtract).then_inc(mix_lo_ready[k], 1)

            in_stats_tile(0, 0)
            in_stats_tile(0, 1)
            variance(0, 0, (0, 1))
            in_stats_tile(0, 2)
            shift_before(0, (0, 1), 1)
            in_stats_tile(0, 3)
            variance(0, 0, (2, 3))
            sum_blocks(0)
            shift_before(0, (2, 3), 2)
            keep_blocks(0)
            sum_blocks(1)
            xT_low(0, 0, (0,))
            keep_blocks(1)
            sum_blocks(2)
            sum_blocks(3)
            mix_low(0)
            keep_blocks(2)
            keep_blocks(3)
            xT_low(0, 0, (1, 2, 3))
            mix_low(1)
            stats_before(1)
            scale_before(1)
            xT_low(1, 0)
            for q in ((0, 1), (2, 3)):
                for t in q:
                    result_stats(0, t)
                variance(1, 0, q)
            for h, q in enumerate(((0, 1), (2, 3))):
                dve.wait_ge(out_rstd, h + 1)
                for t in q:
                    V.scalar_tensor_tensor(out=x[:, t], in0=z[:, t], scalar=rstd[:, 1, t:t + 1], in1=x[:, t],
                                           op0=ALU.mult, op1=ALU.add).then_inc(x_updated, 1)
                for t in q:
                    if h == 1 and t == 2:
                        shift_before(2, (0, 1), in_count(1) + 1)
                    in_stats_tile(2, t)
                variance(0, 2, q)
            V.scalar_tensor_tensor(out=neg_mr[:], in0=mv[:, 1, :, 0], scalar=-1.0, in1=rstd[:, 1],
                                   op0=ALU.mult, op1=ALU.mult).then_inc(out_nmr, 1)
            dve.wait_ge(y_ready, 4 * 2 + 2)
            scale_before(2, (2, 3))
            xT_low(2, 0)
            dve.wait_ge(bias_loaded, 16 * 6)
            ffn(0)
            ffn(1)
            attention(0)
            attention(1)
            ffn(2)
            ffn(3)
            def shift_first_pair():
                dve.wait_ge(out_rstd, out_count(6) + 1)
                V.scalar_tensor_tensor(out=neg_mr[:, 0:2], in0=mv[:, 1, 0:2, 0], scalar=-1.0, in1=rstd[:, 1, 0:2],
                                       op0=ALU.mult, op1=ALU.mult).then_inc(out_nmr, 1)

            early_result(2)
            result_stats(7, 0)
            result_stats(7, 1)
            variance(1, 7, (0, 1))
            truncate_result(7, 1, shift_first_pair)
            result_stats(7, 2)
            result_stats(7, 3)
            variance(1, 7, (2, 3))
            for t in (2, 3):
                V.tensor_scalar(z[:, t], z[:, t], mv[:, 1, t, 0:1], None, ALU.subtract).then_inc(centred, 1)
            dve.wait_ge(out_rstd, out_count(7))
            for t in (2, 3):
                dve.wait_ge(centred, t - 1)
                V.scalar_tensor_tensor(out=x[:, TT + t], in0=z[:, t], scalar=rstd[:, 1, t:t + 1], in1=x[:, TT + t],
                                       op0=ALU.mult, op1=ALU.add).then_inc(x_updated, 1)

        @block.tensor
        def _(pe):
            def product(dst, w, m, start, stop):
                terms = [(a, b) for a, b in ((w[0], m[0]), (w[0], m[1]), (w[1], m[0])) if a is not None and b is not None]
                for q, (a, b) in enumerate(terms):
                    ins = nc.tensor.matmul(dst, a, b, start=start and q == 0, stop=stop and q == len(terms) - 1)
                return ins

            def products(dst, terms, low_ready, w_low_ready=None):
                for q, (w, m) in enumerate(terms):
                    nc.tensor.matmul(dst, w[0], m[0], start=q == 0, stop=False)
                    if w_low_ready is None:
                        nc.tensor.matmul(dst, w[1], m[0], start=False, stop=False)
                if w_low_ready is not None:
                    w_low_ready()
                    for w, m in terms:
                        nc.tensor.matmul(dst, w[1], m[0], start=False, stop=False)
                low_ready()
                for q, (w, m) in enumerate(terms):
                    ins = nc.tensor.matmul(dst, w[0], m[1], start=False, stop=q == len(terms) - 1)
                return ins

            def transposes(n, r, free=None, tiles=range(TT)):
                for t in tiles:
                    m = 4 * n + t
                    pe.wait_ge(y_ready, m + 1)
                    if free:
                        free(t)
                    for k in range(KC):
                        ins = nc.tensor.transpose(bank(r + t)[:, tok(k)], y[:, t, tok(k)], ident[:])
                    ins.then_inc(transposed, 1)

            def linear(n, w_hi, w_lo, between):
                s = n % 2
                for k in range(KC):
                    if n == 0:
                        pe.wait_ge(mix_lo_ready[k], 1)
                    for t in range(TT):
                        if (k, t) in between:
                            between[k, t]()
                        if k == 0:
                            pe.wait_ge(xT_lo_ready, 4 * n + t + 1)
                            if n == 0:
                                pe.wait_ge(keep_ready, t + 1)
                            wait_acc_free(pe, n, t)
                        ins = product(acc[:, t], (xT_hi[:, s, k, tok(t)], xT_lo[:, s, k, tok(t)]),
                                      (w_hi[:, k], w_lo[:, k]), k == 0, k == KC - 1)
                        if k == KC - 1:
                            ins.then_inc(acc_ready, 1)

            def gate_up(s, g, par, b, ring_used=True, first_of=None, c=slice(0, SEQ), tile=None):
                if first_of is not None:
                    pe.wait_ge(xT_hi_ready, 4 * first_of + TT)
                pe.wait_ge(wgu_lo_ready, (g if tile is None else tile) + 1)
                for a, (used, ready) in enumerate(((silu_done, gate_ready), (prod_ready, up_ready))):
                    if ring_used:
                        pe.wait_ge(used, g - 1)
                    if first_of is not None:
                        pe.wait_ge(xT_lo_ready, 4 * first_of + a + 1)
                    terms = [((wgu_hi[:, par, a, k], wgu_lo[:, par, a, k]), (xT_hi[:, s, k, c], xT_lo[:, s, k, c]))
                             for k in range(KC)]

                    def low_ready():
                        if first_of is not None:
                            pe.wait_ge(xT_lo_ready, 4 * first_of + TT)

                    products(bank(b + a)[:, c], terms, low_ready).then_inc(ready, 1)

            def down(layer, n, g, par, start=False, stop=False, tiles=range(TT), tile=None):
                pe.wait_ge(g_ready, g + 1)
                pe.wait_ge(wd_lo_ready, (g if tile is None else tile) + 1)
                for t in tiles:
                    if start:
                        wait_acc_free(pe, n, t)
                    low = g_lo[:, par, tok(t)] if layer == 0 else None
                    ins = product(acc[:, t], (g_hi[:, par, tok(t)], low), (wd_hi[:, par], wd_lo[:, par]), start, stop)
                    if stop:
                        ins.then_inc(acc_ready, 1)
                if not stop and tile is None:
                    ins.then_inc(down_done, 1)

            def ffn(p):
                s, g0, layer = p % NSTREAM, NI * p, p // NSTREAM
                n = (2 if layer == 0 else 6) + s
                r0 = pass_bank(p)

                def gu(i, j=0, used=True, first_of=None):
                    gate_up(s, 2 * j + (g0 + i) if not isinstance(j, int) else g0 + i, (g0 + i) % 2, r0 + 2 * i, used,
                            first_of)

                def dn(i, j=0, **kw):
                    down(layer, n, 2 * j + (g0 + i) if not isinstance(j, int) else g0 + i, (g0 + i) % 2, **kw)

                gu(0, used=False, first_of=n)
                gu(1, used=False)
                gu(2)
                dn(0, start=True)
                last = p == NPASS - 1
                with pe.Fori(0, (NI - 3) // 2 - last) as j:
                    for h in range(2):
                        gu(3 + h, j)
                        dn(1 + h, j)
                if last:
                    def gu_half(q):
                        i, h = halves[q]
                        gate_up(s, g0 + NI - 2 + q, (g0 + i) % 2, r0 + 2 * i, c=half(h), tile=g0 + i)

                    def dn_half(q):
                        i, h = halves[q]
                        down(layer, n, g0 + NI - 2 + q, (g0 + i) % 2, stop=i == NI - 1,
                             tiles=(2 * h, 2 * h + 1), tile=g0 + i)

                    gu_half(0)
                    dn(NI - 4)
                    gu_half(1)
                    dn(NI - 3)
                    gu_half(2)
                    dn_half(0)
                    dn_half(1)
                    gu_half(3)
                    dn_half(2)
                    dn_half(3)
                    return
                dn(NI - 2)
                if n_in[p] is not None:
                    def free(t):
                        g = g0 + NI - 2 + t // 2
                        pe.wait_ge(silu_done if t % 2 == 0 else prod_ready, g + 1)
                    transposes(n_in[p], r0 + 2 * NI, free)
                dn(NI - 1, stop=True)

            def attention(s):
                r, n = pass_bank(2), 4 + s

                def v_tile(t):
                    for k in range(KC):
                        ins = product(bank(r + 2)[:, tok(t)], (xT_hi[:, s, k, tok(t)], xT_lo[:, s, k, tok(t)]),
                                      (wqkv_hi[:, k, tok(2)], wqkv_lo[:, k, tok(2)]), k == 0, k == KC - 1)
                    return ins

                def prob_transpose(t):
                    pe.wait_ge(exp_done, 4 * s + t + 1)
                    for k in range(KC):
                        ins = nc.tensor.transpose(bank(r + 3 + t)[:, tok(k)], prob[:, t, tok(k)], ident[:])
                    ins.then_inc(prob_transposed, 1)

                def mix(h):
                    q = half(h)
                    pe.wait_ge(pT_hi_ready, 4 * s + 2 * h + 2)
                    pe.wait_ge(exp_done, 4 * s + TT)
                    pe.wait_ge(v_hi_ready, 2 * s + 2)
                    products(acc[:, 3 - h, q],
                             [((qkv_hi[:, 2, tok(k)], qkv_lo[:, 2, tok(k)]), (wide_hi[:, k, q], wide_lo[:, k, q]))
                              for k in range(KC)],
                             lambda: pe.wait_ge(pT_lo_ready, 4 * s + 2 * h + 2),
                             lambda: pe.wait_ge(v_lo_ready, 2 * s + 2)).then_inc(mixed, 1)

                def project(t):
                    oT, w = (qkv_hi[:, 0, tok(t)], qkv_lo[:, 0, tok(t)]), (wo_hi[:], wo_lo[:])
                    pe.wait_ge(oT_hi_ready, 2 * s + t // 2 + 1)
                    if t >= 2:
                        pe.wait_ge(oT_lo_ready, 2 * s + 4 - t)
                    nc.tensor.matmul(acc[:, t], oT[0], w[0], start=True, stop=False)
                    nc.tensor.matmul(acc[:, t], oT[0], w[1], start=False, stop=False)
                    pe.wait_ge(oT_lo_ready, 2 * s + t // 2 + 1)
                    nc.tensor.matmul(acc[:, t], oT[1], w[0], start=False, stop=True).then_inc(acc_ready, 1)

                pe.wait_ge(attw_lo_ready, 2)
                pe.wait_ge(xT_hi_ready, 4 * n + TT)
                for q, a in enumerate((1, 0)):
                    pe.wait_ge(xT_lo_ready, 4 * n + q + 1)
                    products(bank(r + q),
                             [((wqkv_hi[:, k, tok(a)], wqkv_lo[:, k, tok(a)]), (xT_hi[:, s, k], xT_lo[:, s, k]))
                              for k in range(KC)],
                             lambda: pe.wait_ge(xT_lo_ready, 4 * n + TT)).then_inc(qk_prod, 1)
                v_tile(0)
                v_tile(1).then_inc(v_prod, 1)
                pe.wait_ge(qk_lo_ready, 2 * s + 2)
                for t in range(TT):
                    wait_acc_free(pe, n, t)
                    product(acc[:, t], (qkv_hi[:, 0, tok(t)], qkv_lo[:, 0, tok(t)]),
                            (qkv_hi[:, 1], qkv_lo[:, 1]), True, True).then_inc(scored, 1)
                pe.wait_ge(v_full, 2 * s + 1)
                v_tile(2)
                v_tile(3).then_inc(v_prod, 1)
                prob_transpose(0)
                prob_transpose(1)
                prob_transpose(2)
                pe.wait_ge(v_full, 2 * s + 2)
                prob_transpose(3)
                mix(0)
                mix(1)
                project(0)
                pe.wait_ge(pT_lo_ready, 4 * s + TT)
                transposes(n + 1, r, tiles=(0, 1))
                project(1)
                transposes(n + 1, r, tiles=(2, 3))
                project(2)
                project(3)

            def spread_blocks(k):
                pe.wait_ge(blk_summed, k + 1)
                nc.tensor.matmul(acc[:, k, 0:D // BLK], ones_blk[:], blk_rows[:, k], start=True,
                                 stop=True).then_inc(blk_spread, 1)

            pe.wait_ge(zeros_set, 1)
            for _ in range(WARM_UP):
                nc.tensor.matmul(acc[:, TT - 1], sgn[:, 0:P], sgn[:], start=True, stop=True)
            pe.wait_ge(ident_loaded, 16)
            for t in range(TT):
                transposes(0, 0, tiles=(t,))
                if t == 0:
                    pe.wait_ge(ones_loaded, 16)
                spread_blocks(t)
            linear(0, wide_hi, wide_lo, {(KC - 1, 0): lambda: transposes(1, 0)})

            def transpose_pair(q):
                pe.wait_ge(xT_lo_ready, 8)
                transposes(2, 0, tiles=q)

            linear(1, wide_hi, wide_lo, {(KC - 1, 0): lambda: transpose_pair((0, 1)),
                                         (KC - 1, 2): lambda: transpose_pair((2, 3))})
            ffn(0)
            ffn(1)
            attention(0)
            attention(1)
            ffn(2)
            ffn(3)


def kernel(L0_attn_data, L0_attn_weight, L0_attn_mask, L0_ffn_w_gate, L0_ffn_b_gate, L0_ffn_w_up, L0_ffn_b_up,
           L0_ffn_w_down, L0_ffn_b_down, L1_attn_Wqkv, L1_attn_bqkv, L1_attn_Wo, L1_attn_bo, L1_ffn_w_gate,
           L1_ffn_w_up, L1_ffn_w_down):
    import concourse.bacc as bacc
    from concourse.bass_utils import run_bass_kernel_spmd

    def chunked(w):
        return np.asarray(w).reshape(KC, P, -1).transpose(1, 0, 2)

    def padded(w):
        w = np.asarray(w)
        return np.concatenate([w, np.zeros((NI * P - INTER,) + w.shape[1:], w.dtype)])

    def by_feature(w):
        return padded(w).reshape(NI, P, KC, P).transpose(0, 3, 2, 1)

    def columns(b):
        return padded(b).reshape(NI, P).T

    def rows(b):
        b = np.asarray(b)
        return np.broadcast_to(b, (P, b.size))

    bqkv = np.asarray(L1_attn_bqkv)
    gu = np.stack([np.stack([by_feature(a), by_feature(b)], axis=2)
                   for a, b in ((L0_ffn_w_gate, L0_ffn_w_up), (L1_ffn_w_gate, L1_ffn_w_up))])
    arrays = {
        "x_in": np.asarray(L0_attn_data).reshape(NSTREAM * TT, P, D),
        "w_mix": chunked(np.asarray(L0_attn_weight).T),
        "mask": chunked(np.asarray(L0_attn_mask).T),
        "ffn_gu": gu.reshape(2, NI, P, 2 * KC * P),
        "ffn_d": np.stack([padded(np.asarray(w).T).reshape(NI, P, D) for w in (L0_ffn_w_down, L1_ffn_w_down)]),
        "b_gate": columns(L0_ffn_b_gate),
        "b_up": columns(L0_ffn_b_up),
        "b_down": rows(L0_ffn_b_down),
        "w_qkv": chunked(L1_attn_Wqkv).reshape(P, KC * 3 * P),
        "b_qk": bqkv[:2 * P].reshape(2, P).T,
        "b_v": rows(bqkv[2 * P:]),
        "w_o": np.asarray(L1_attn_Wo),
        "b_o": rows(L1_attn_bo),
        "identity": np.eye(P, dtype=np.float32),
        "block_ones": np.kron(np.eye(P // BLK, dtype=np.float32), np.ones((BLK, BLK), np.float32)),
    }
    arrays = {f"{k}_dram": np.ascontiguousarray(a) for k, a in arrays.items()}
    nc = bacc.Bacc("TRN2", target_bir_lowering=False, num_devices=1)
    args = [nc.dram_tensor(k, a.shape, mybir.dt.from_np(a.dtype), kind="ExternalInput").ap()
            for k, a in arrays.items()]
    args.append(nc.dram_tensor("out_dram", (NSTREAM * TT, P, D), F32, kind="ExternalOutput").ap())
    build_two_layers(nc, *args)
    r = run_bass_kernel_spmd(nc, [arrays], core_ids=[0])
    return r.results[0]["out_dram"].reshape(NSTREAM, SEQ, D)
```
